# Optimizing a Trainium2 kernel written in Bass

```python
import numpy as np
import jax
import jax.numpy as jnp

def _softmax(x, axis=-1):
    return jax.nn.softmax(x, axis=axis)

def _gelu(x):
    return jax.nn.gelu(x, approximate=True)

def _silu(x):
    return jax.nn.silu(x)

def _sigmoid(x):
    return jax.nn.sigmoid(x)

def _layernorm(x, axis=-1, eps=1e-05):
    m = jnp.mean(x, axis=axis, keepdims=True)
    v = jnp.var(x, axis=axis, keepdims=True)
    return (x - m) / jnp.sqrt(v + eps)

def _scatter_add(tgt, idx, src, axis=0):
    return tgt.at[idx].add(src)

def _segment_sum(src, seg, n):
    return jax.ops.segment_sum(src, seg, n)
kernel_name = 'mk_recurrent_d2_jaxref_r4_07682f'

def setup_inputs(seed: int=0):
    np.random.seed(seed)
    _w = jnp.asarray

    def _L0_attn_setup():
        import jax, jax.numpy as jnp
        import numpy as np
        D = 256
        K_LOW1 = D // 4
        K_LOW2 = D // 4

        def mix_precision_matmul(x, w):
            d = x.shape[-1]
            w1 = w[:K_LOW1]
            wh = w[K_LOW1:d - K_LOW2]
            w2 = w[d - K_LOW2:]
            y1 = jnp.matmul(x[..., :K_LOW1].astype(jnp.float16), w1.astype(jnp.float16)).astype(jnp.float32)
            yh = jnp.matmul(x[..., K_LOW1:d - K_LOW2], wh)
            y2 = jnp.matmul(x[..., d - K_LOW2:].astype(jnp.float16), w2.astype(jnp.float16)).astype(jnp.float32)
            return y1 + yh + y2
        key = jax.random.key(seed)
        k1, k2, k3, k4 = jax.random.split(key, 4)
        B, N, d = (8, 512, D)
        x = jax.random.normal(k1, (B, N, d), dtype=jnp.float32)
        weight_qkv = jax.random.normal(k2, (d, 3 * d), dtype=jnp.float32) * d ** (-0.5)
        out_w = jax.random.normal(k3, (d, d), dtype=jnp.float32) * d ** (-0.5)
        out_b = jax.random.normal(k4, (d,), dtype=jnp.float32) * 0.01
        return {'x': x, 'weight_qkv': weight_qkv, 'out_w': out_w, 'out_b': out_b}
    _L0_attn_in = _L0_attn_setup()

    def _L0_ffn_setup():
        import jax, jax.numpy as jnp
        import numpy as np

        def _binarize(w):
            alpha = jax.lax.stop_gradient(jnp.mean(jnp.abs(w), axis=1, keepdims=True))
            bw = alpha * jnp.sign(w)
            return w + jax.lax.stop_gradient(bw - w)
        key = jax.random.key(seed)
        k1, k2, k3, k4, k5 = jax.random.split(key, 5)
        D, H = (256, 1024)
        x = jax.random.normal(k1, (64, 196, D), dtype=jnp.float32)
        w1 = jax.random.normal(k2, (H, D), dtype=jnp.float32) * 0.02
        b1 = jax.random.normal(k3, (H,), dtype=jnp.float32) * 0.02
        w2 = jax.random.normal(k4, (D, H), dtype=jnp.float32) * 0.02
        b2 = jax.random.normal(k5, (D,), dtype=jnp.float32) * 0.02
        return {'x': x, 'w1': w1, 'b1': b1, 'w2': w2, 'b2': b2}
    _L0_ffn_in = _L0_ffn_setup()

    def _L1_attn_setup():
        import jax, jax.numpy as jnp
        import numpy as np
        B_, L_, D_RES, D_INNER, N_STATE, K_CONV = (2, 256, 256, 128, 64, 3)

        def _causal_dwconv(x, w, b):
            xt = jnp.transpose(x, (0, 2, 1))
            k = w.shape[-1]
            out = jax.lax.conv_general_dilated(xt, w, (1,), [(k - 1, 0)], feature_group_count=w.shape[0])
            return jnp.transpose(out, (0, 2, 1)) + b

        def _s6(u, W_delta, b_delta, W_B, W_C, A_log, D):
            A = -jnp.exp(A_log)
            delta = jax.nn.softplus(u @ W_delta + b_delta)
            Bm = u @ W_B
            Cm = u @ W_C

            def step(h, inputs):
                u_t, d_t, b_t, c_t = inputs
                dA = jnp.exp(d_t[..., None] * A)
                h = dA * h + (d_t * u_t)[..., None] * b_t[:, None, :]
                y = jnp.einsum('bdn,bn->bd', h, c_t)
                return (h, y)
            h0 = jnp.zeros((u.shape[0], A.shape[0], A.shape[1]), u.dtype)
            xs = (jnp.swapaxes(u, 0, 1), jnp.swapaxes(delta, 0, 1), jnp.swapaxes(Bm, 0, 1), jnp.swapaxes(Cm, 0, 1))
            _, ys = jax.lax.scan(step, h0, xs)
            return jnp.swapaxes(ys, 0, 1) + u * D
        key = jax.random.key(seed)
        ks = jax.random.split(key, 8)
        s = lambda k, shp, sc: jax.random.normal(k, shp, dtype=jnp.float32) * sc
        return {'x': s(ks[0], (B_, L_, D_RES), 1.0), 'ln_gamma': jnp.ones((D_RES,), jnp.float32), 'ln_beta': jnp.zeros((D_RES,), jnp.float32), 'W_up': s(ks[1], (D_RES, 2 * D_INNER), 0.02), 'b_up': jnp.zeros((2 * D_INNER,), jnp.float32), 'conv_w': s(ks[2], (D_INNER, 1, K_CONV), 0.2), 'conv_b': jnp.zeros((D_INNER,), jnp.float32), 'W_delta': s(ks[3], (D_INNER, D_INNER), 0.02), 'b_delta': jnp.full((D_INNER,), -4.0, jnp.float32), 'W_B': s(ks[4], (D_INNER, N_STATE), 0.02), 'W_C': s(ks[5], (D_INNER, N_STATE), 0.02), 'A_log': jnp.log(jnp.broadcast_to(jnp.arange(1, N_STATE + 1, dtype=jnp.float32), (D_INNER, N_STATE))).copy(), 'D': jnp.ones((D_INNER,), jnp.float32), 'W_down': s(ks[6], (D_INNER, D_RES), 0.02), 'b_down': jnp.zeros((D_RES,), jnp.float32)}
    _L1_attn_in = _L1_attn_setup()

    def _L1_ffn_setup():
        import jax, jax.numpy as jnp
        import numpy as np
        B, S, D = (4, 1024, 256)
        E, F_EXP = (16, 512)
        F_C = 2.0
        F_SH = 512
        key = jax.random.key(seed)
        ks = jax.random.split(key, 8)
        s = 0.02
        return {'hidden_states': jax.random.normal(ks[0], (B, S, D), jnp.float32), 'gate_w': jax.random.normal(ks[1], (E, D), jnp.float32) * s, 'Wg': jax.random.normal(ks[2], (E, F_EXP, D), jnp.float32) * s, 'Wu': jax.random.normal(ks[3], (E, F_EXP, D), jnp.float32) * s, 'Wd': jax.random.normal(ks[4], (E, D, F_EXP), jnp.float32) * s, 'Ws_g': jax.random.normal(ks[5], (F_SH, D), jnp.float32) * s, 'Ws_u': jax.random.normal(ks[6], (F_SH, D), jnp.float32) * s, 'Ws_d': jax.random.normal(ks[7], (D, F_SH), jnp.float32) * s}
    _L1_ffn_in = _L1_ffn_setup()
    _d = {'L0_attn_x': _L0_attn_in['x'], 'L0_attn_weight_qkv': _L0_attn_in['weight_qkv'], 'L0_attn_out_w': _L0_attn_in['out_w'], 'L0_attn_out_b': _L0_attn_in['out_b'], 'L0_ffn_w1': _L0_ffn_in['w1'], 'L0_ffn_b1': _L0_ffn_in['b1'], 'L0_ffn_w2': _L0_ffn_in['w2'], 'L0_ffn_b2': _L0_ffn_in['b2'], 'L1_attn_ln_gamma': _L1_attn_in['ln_gamma'], 'L1_attn_ln_beta': _L1_attn_in['ln_beta'], 'L1_attn_W_up': _L1_attn_in['W_up'], 'L1_attn_b_up': _L1_attn_in['b_up'], 'L1_attn_conv_w': _L1_attn_in['conv_w'], 'L1_attn_conv_b': _L1_attn_in['conv_b'], 'L1_attn_W_delta': _L1_attn_in['W_delta'], 'L1_attn_b_delta': _L1_attn_in['b_delta'], 'L1_attn_W_B': _L1_attn_in['W_B'], 'L1_attn_W_C': _L1_attn_in['W_C'], 'L1_attn_A_log': _L1_attn_in['A_log'], 'L1_attn_D': _L1_attn_in['D'], 'L1_attn_W_down': _L1_attn_in['W_down'], 'L1_attn_b_down': _L1_attn_in['b_down'], 'L1_ffn_gate_w': _L1_ffn_in['gate_w'], 'L1_ffn_Wg': _L1_ffn_in['Wg'], 'L1_ffn_Wu': _L1_ffn_in['Wu'], 'L1_ffn_Wd': _L1_ffn_in['Wd'], 'L1_ffn_Ws_g': _L1_ffn_in['Ws_g'], 'L1_ffn_Ws_u': _L1_ffn_in['Ws_u'], 'L1_ffn_Ws_d': _L1_ffn_in['Ws_d']}
    _x0 = _d['L0_attn_x']
    _d['L0_attn_x'] = jax.random.normal(jax.random.fold_in(jax.random.key(seed), 1), (2, 4096, 256), dtype=_x0.dtype)
    del _x0
    return _d

def reference(L0_attn_x, L0_attn_weight_qkv, L0_attn_out_w, L0_attn_out_b, L0_ffn_w1, L0_ffn_b1, L0_ffn_w2, L0_ffn_b2, L1_attn_ln_gamma, L1_attn_ln_beta, L1_attn_W_up, L1_attn_b_up, L1_attn_conv_w, L1_attn_conv_b, L1_attn_W_delta, L1_attn_b_delta, L1_attn_W_B, L1_attn_W_C, L1_attn_A_log, L1_attn_D, L1_attn_W_down, L1_attn_b_down, L1_ffn_gate_w, L1_ffn_Wg, L1_ffn_Wu, L1_ffn_Wd, L1_ffn_Ws_g, L1_ffn_Ws_u, L1_ffn_Ws_d):

    def _L0_attn_ref(x, weight_qkv, out_w, out_b):
        import jax, jax.numpy as jnp
        import numpy as np
        D = 256
        K_LOW1 = D // 4
        K_LOW2 = D // 4

        def mix_precision_matmul(x, w):
            d = x.shape[-1]
            w1 = w[:K_LOW1]
            wh = w[K_LOW1:d - K_LOW2]
            w2 = w[d - K_LOW2:]
            y1 = jnp.matmul(x[..., :K_LOW1].astype(jnp.float16), w1.astype(jnp.float16)).astype(jnp.float32)
            yh = jnp.matmul(x[..., K_LOW1:d - K_LOW2], wh)
            y2 = jnp.matmul(x[..., d - K_LOW2:].astype(jnp.float16), w2.astype(jnp.float16)).astype(jnp.float32)
            return y1 + yh + y2
        d = x.shape[-1]
        qkv = mix_precision_matmul(x, weight_qkv)
        q, k, v = jnp.split(qkv, 3, axis=-1)
        q = q / jnp.sqrt(jnp.asarray(d, dtype=q.dtype))
        qk = jnp.einsum('bqd,bkd->bqk', q, k)
        s = jax.nn.softmax(qk, axis=-1)
        y = jnp.einsum('bqk,bkd->bqd', s, v)
        return jnp.matmul(y, out_w.T) + out_b

    def _L0_ffn_ref(x, w1, b1, w2, b2):
        import jax, jax.numpy as jnp
        import numpy as np

        def _binarize(w):
            alpha = jax.lax.stop_gradient(jnp.mean(jnp.abs(w), axis=1, keepdims=True))
            bw = alpha * jnp.sign(w)
            return w + jax.lax.stop_gradient(bw - w)
        bw1 = _binarize(w1)
        h = jnp.einsum('bsd,hd->bsh', x, bw1) + b1
        h = jax.nn.gelu(h, approximate=False)
        bw2 = _binarize(w2)
        out = jnp.einsum('bsh,dh->bsd', h, bw2) + b2
        return out

    def _L1_attn_ref(x, ln_gamma, ln_beta, W_up, b_up, conv_w, conv_b, W_delta, b_delta, W_B, W_C, A_log, D, W_down, b_down):
        import jax, jax.numpy as jnp
        import numpy as np
        B_, L_, D_RES, D_INNER, N_STATE, K_CONV = (2, 256, 256, 128, 64, 3)

        def _causal_dwconv(x, w, b):
            xt = jnp.transpose(x, (0, 2, 1))
            k = w.shape[-1]
            out = jax.lax.conv_general_dilated(xt, w, (1,), [(k - 1, 0)], feature_group_count=w.shape[0])
            return jnp.transpose(out, (0, 2, 1)) + b

        def _s6(u, W_delta, b_delta, W_B, W_C, A_log, D):
            A = -jnp.exp(A_log)
            delta = jax.nn.softplus(u @ W_delta + b_delta)
            Bm = u @ W_B
            Cm = u @ W_C

            def step(h, inputs):
                u_t, d_t, b_t, c_t = inputs
                dA = jnp.exp(d_t[..., None] * A)
                h = dA * h + (d_t * u_t)[..., None] * b_t[:, None, :]
                y = jnp.einsum('bdn,bn->bd', h, c_t)
                return (h, y)
            h0 = jnp.zeros((u.shape[0], A.shape[0], A.shape[1]), u.dtype)
            xs = (jnp.swapaxes(u, 0, 1), jnp.swapaxes(delta, 0, 1), jnp.swapaxes(Bm, 0, 1), jnp.swapaxes(Cm, 0, 1))
            _, ys = jax.lax.scan(step, h0, xs)
            return jnp.swapaxes(ys, 0, 1) + u * D
        mu = jnp.mean(x, -1, keepdims=True)
        var = jnp.mean((x - mu) ** 2, -1, keepdims=True)
        y = (x - mu) * jax.lax.rsqrt(var + 1e-05) * ln_gamma + ln_beta
        up = y @ W_up + b_up
        left, right = jnp.split(up, 2, axis=-1)
        left = jax.nn.silu(_causal_dwconv(left, conv_w, conv_b))
        left = _s6(left, W_delta, b_delta, W_B, W_C, A_log, D)
        gated = left * jax.nn.silu(right)
        return x + gated @ W_down + b_down

    def _L1_ffn_ref(hidden_states, gate_w, Wg, Wu, Wd, Ws_g, Ws_u, Ws_d):
        import jax, jax.numpy as jnp
        import numpy as np
        B, S, D = (4, 1024, 256)
        E, F_EXP = (16, 512)
        F_C = 2.0
        F_SH = 512
        b, s, d = hidden_states.shape
        e = gate_w.shape[0]
        cap = int(s * F_C / e)
        logits = jnp.einsum('bsd,ed->bse', hidden_states, gate_w)
        scores = jax.nn.softmax(logits, axis=-1).transpose(0, 2, 1)
        topk_w, topk_idx = jax.lax.top_k(scores, cap)
        x_tok = jnp.take_along_axis(hidden_states[:, None, :, :], topk_idx[..., None], axis=2)
        g = jnp.einsum('becd,efd->becf', x_tok, Wg)
        u = jnp.einsum('becd,efd->becf', x_tok, Wu)
        h = jax.nn.gelu(g, approximate=False) * u
        eo = jnp.einsum('becf,edf->becd', h, Wd) * topk_w[..., None]
        offs = (jnp.arange(b) * s)[:, None, None]
        flat_idx = (topk_idx + offs).reshape(-1)
        flat = jnp.zeros((b * s, d), hidden_states.dtype)
        flat = flat.at[flat_idx].add(eo.reshape(-1, d))
        out = flat.reshape(b, s, d)
        gs = jnp.einsum('bsd,fd->bsf', hidden_states, Ws_g)
        us = jnp.einsum('bsd,fd->bsf', hidden_states, Ws_u)
        shared = jnp.einsum('bsf,df->bsd', jax.nn.gelu(gs, approximate=False) * us, Ws_d)
        return out + shared
    x = L0_attn_x
    xn = _layernorm(x, axis=-1)
    s = _L0_attn_ref(xn, L0_attn_weight_qkv, L0_attn_out_w, L0_attn_out_b)
    g = _silu(_L0_ffn_ref(xn, L0_ffn_w1, L0_ffn_b1, L0_ffn_w2, L0_ffn_b2))
    x = x + s * g
    xn = _layernorm(x, axis=-1)
    s = _L1_attn_ref(xn, L1_attn_ln_gamma, L1_attn_ln_beta, L1_attn_W_up, L1_attn_b_up, L1_attn_conv_w, L1_attn_conv_b, L1_attn_W_delta, L1_attn_b_delta, L1_attn_W_B, L1_attn_W_C, L1_attn_A_log, L1_attn_D, L1_attn_W_down, L1_attn_b_down)
    g = _silu(_L1_ffn_ref(xn, L1_ffn_gate_w, L1_ffn_Wg, L1_ffn_Wu, L1_ffn_Wd, L1_ffn_Ws_g, L1_ffn_Ws_u, L1_ffn_Ws_d))
    x = x + s * g
    return x

_drawn_inputs = setup_inputs


def setup_inputs(seed=0):
    import zlib

    import numpy as np

    out = dict(_drawn_inputs(seed))
    spreads = {'L1_attn_ln_gamma': (1.0, 0.2),
     'L1_attn_ln_beta': (0.0, 0.1),
     'L1_attn_b_up': (0.0, 0.1),
     'L1_attn_conv_b': (0.0, 0.1),
     'L1_attn_b_delta': (-4.0, 0.2),
     'L1_attn_D': (1.0, 0.2),
     'L1_attn_b_down': (0.0, 0.1)}
    factors = {}
    for name, (base, spread) in spreads.items():
        noise = np.random.default_rng([zlib.crc32(name.encode()), seed]).standard_normal(out[name].shape)
        drawn = base * np.exp(spread * noise) if base else spread * noise
        out[name] = jnp.asarray(drawn.astype(out[name].dtype))
    for name, factor in factors.items():
        out[name] = (out[name] * factor).astype(out[name].dtype)
    return out
```

```python
from contextlib import ExitStack

import concourse.bass as bass
from concourse import mybir

F32 = mybir.dt.float32
F32R = mybir.dt.float32r
F16 = mybir.dt.float16
I32 = mybir.dt.int32
U32 = mybir.dt.uint32
ALU = mybir.AluOpType
ACT = mybir.ActivationFunctionType
AX_X = mybir.AxisListType.X

P = 128
BATCH = 2
SEQ = 4096
TOKENS = BATCH * SEQ
D = 256
DC = D // P
GROUP = 512
GT = GROUP // P
GROUPS = SEQ // GROUP
BANK = 512
LN_EPS = 1e-5


class Lane:

    def __init__(self, nc, ctx, name):
        self.nc, self.ctx, self.name = nc, ctx, name
        self.queue = []
        self.waited = {}
        self.stage = 0
        self.fence = []
        self.last = None
        self.new_stage()

    def new_stage(self):
        self.sem = self.ctx.enter_context(self.nc.semaphore(f"{self.name}_done_{self.stage}"))
        self.count = 0
        self.stage += 1

    def _waits(self, waits):
        need = []
        for token in list(self.fence) + list(waits):
            if token is None:
                continue
            sem, value = token
            if self.waited.get(sem.name, (None, 0))[1] < value:
                self.waited[sem.name] = (sem, value)
                need = [n for n in need if n[0].name != sem.name] + [(sem, value)]
        self.fence = []
        return need

    def do(self, issue, *waits, signal=True):
        need = self._waits(waits)
        token = None
        if signal:
            self.count += 1
            token = self.last = (self.sem, self.count)
        self.queue.append((need, issue, self.sem if signal else None, 1))
        return token

    def dma(self, slot_sem, issue, *waits):
        need = self._waits(waits)
        slot_sem.count += 16
        self.queue.append((need, issue, slot_sem.sem, 16))
        return (slot_sem.sem, slot_sem.count)

    def replay(self, engine):
        for need, issue, sem, by in self.queue:
            for wait_sem, value in need:
                engine.wait_ge(wait_sem, value)
            done = issue(engine) if issue is not None else None
            if sem is not None:
                done.then_inc(sem, by)


class DmaSem:
    def __init__(self, core, name):
        self.sem = core.ctx.enter_context(core.nc.semaphore(name))
        self.count = 0
        core.dma_sems.append(self)

    def token(self):
        return (self.sem, self.count)


class Slot:

    def __init__(self, view, dma_sem=None):
        self.view, self.free, self.dma_sem = view, [], dma_sem


class Ring:
    def __init__(self, slots):
        self.slots, self.at = slots, -1

    def take(self):
        self.at += 1
        return self.slots[self.at % len(self.slots)]


class Core:

    def __init__(self, nc, ctx):
        self.nc, self.ctx, self.dma_sems = nc, ctx, []
        self.pe = Lane(nc, ctx, "pe")
        self.act = Lane(nc, ctx, "act")
        self.dve = Lane(nc, ctx, "dve")
        self.pool = Lane(nc, ctx, "pool")
        self.sp = Lane(nc, ctx, "sp")
        self.lanes = [self.pe, self.act, self.dve, self.pool, self.sp]

    def psum_banks(self, ctx, stage):
        return [ctx.enter_context(self.nc.psum_tensor(f"{stage}_bank{i}", [P, BANK], F32)) for i in range(8)]

    def sb(self, ctx, name, shape, dtype):
        return ctx.enter_context(self.nc.sbuf_tensor(f"{name}_sb", shape, dtype))

    def dma_ring(self, ctx, name, n, shape, dtype):
        return Ring([Slot(self.sb(ctx, f"{name}{i}", shape, dtype), DmaSem(self, f"{name}_dma{i}")) for i in range(n)])

    def ring(self, ctx, name, n, shape, dtype):
        return Ring([Slot(self.sb(ctx, f"{name}{i}", shape, dtype)) for i in range(n)])

    def hand_over(self):
        every = [lane.last for lane in self.lanes if lane.last] + [d.token() for d in self.dma_sems if d.count]
        for lane in self.lanes:
            lane.fence = list(every)
            lane.new_stage()
            lane.last = None

    def run(self):
        block = self.ctx.enter_context(self.nc.Block())
        block.tensor(self.pe.replay)
        block.scalar(self.act.replay)
        block.vector(self.dve.replay)
        block.gpsimd(self.pool.replay)
        block.sync(self.sp.replay)


def f32(view):
    return view.bitcast(F32)


def split_weights(core, src, hi, lo, *waits):
    th = core.dve.do(lambda e: e.tensor_copy(hi, src), *waits)
    return core.dve.do(lambda e: e.tensor_tensor(lo, src, f32(hi), ALU.subtract), th)


def split_weights_on_pool(core, src, hi, lo, *waits):
    th = core.pool.do(lambda e: e.tensor_scalar(hi, src, 1.0, 0.0, ALU.mult, ALU.add), *waits)
    return core.pool.do(lambda e: e.tensor_tensor(lo, src, f32(hi), ALU.subtract), th)


def split_from_psum(core, bank, hi, lo, matmul_done, *free, scale=1.0):
    assert scale == 1.0
    th = core.act.do(lambda e: e.activation(hi, bank, ACT.Copy), matmul_done, *free)
    return core.dve.do(lambda e: e.tensor_tensor(lo, bank, f32(hi), ALU.subtract), th, *free)


class Constants:
    def __init__(self, core, ctx):
        nc, pool = core.nc, core.pool
        self.identity = core.sb(ctx, "identity", [P, P], F32)
        self.ones = core.sb(ctx, "ones", [P, P], F32)
        self.minus_half = core.sb(ctx, "minus_half", [P, GT], F32)
        t = pool.do(lambda e: e.memset(self.identity[:, :], 0.0))
        pool.do(lambda e: e.memset(self.ones[:, :], 1.0))
        pool.do(lambda e: e.memset(self.minus_half[:, :], -0.5))
        self.ready = pool.do(lambda e: e.affine_select(
            out=self.identity[:, :], in_=self.identity[:, :], compare_op=ALU.not_equal, fill=1.0,
            base=0, pattern=[[-1, P]], channel_multiplier=1), t)


class LayerNorm:

    def __init__(self, core, ctx, consts, name, n=2):
        self.core, self.consts = core, consts
        self.stats = core.ring(ctx, f"{name}_stats", n, [P, GT, 6], F32)
        self.moments = core.ring(ctx, f"{name}_moments", n, [P, GT, 2], F32)
        self.rstd = core.ring(ctx, f"{name}_rstd", n, [P, 2, GT], F32)

    def __call__(self, src, dst, tiles, src_ready, *dst_free):
        core, consts = self.core, self.consts
        st, mo, rs = self.stats.take(), self.moments.take(), self.rstd.take()
        free = list(st.free)
        aggr = None
        for j in range(tiles):
            t = core.dve.do(lambda e, j=j: e.bn_stats(st.view[:, j, :], src[j]), src_ready, *free)
            aggr = core.dve.do(lambda e, j=j: e.bn_aggr(mo.view[:, j, :], st.view[:, j, :]), t)
        ve, r = rs.view[:, 0, 0:tiles], rs.view[:, 1, 0:tiles]
        t = core.pool.do(lambda e: e.tensor_scalar(ve, mo.view[:, 0:tiles, 1], LN_EPS, None, ALU.add), aggr, *free)
        t = core.pool.do(lambda e: e.tensor_tensor(r, ve, consts.minus_half[:, 0:tiles], ALU.pow), t, consts.ready)
        for j in range(tiles):
            last = core.dve.do(lambda e, j=j: e.tensor_scalar(
                dst[j], src[j], mo.view[:, j, 0:1], rs.view[:, 1, j:j + 1], ALU.subtract, ALU.mult), t, *dst_free)
        st.free = [last]
        return last


def binary_ffn_and_qkv(core, consts, w, kv, b, x_dram, q_dram, g_dram):
    with ExitStack() as ctx:
        banks = core.psum_banks(ctx, f"ffn{b}")
        tr_ring = Ring([Slot(banks[0][:, :]), Slot(banks[1][:, :])])
        mm_ring = Ring([Slot(banks[2][:, :]), Slot(banks[3][:, :])])
        hid_ring = Ring([Slot(banks[4][:, :]), Slot(banks[5][:, :])])
        out_banks = [Slot(banks[6][:, :]), Slot(banks[7][:, :])]
        x_ring = core.dma_ring(ctx, f"x_b{b}_", 2, [P, GT, D], F32)
        xt_hi = core.ring(ctx, f"xt_hi_b{b}_", 2, [P, DC, GROUP], F32R)
        xt_lo = core.ring(ctx, f"xt_lo_b{b}_", 2, [P, DC, GROUP], F32R)
        xt_16 = core.ring(ctx, f"xt_16_b{b}_", 2, [P, GROUP], F16)
        q_ring = core.dma_ring(ctx, f"q_out_b{b}_", 1, [P, DC, GROUP], F32)
        g_ring = core.dma_ring(ctx, f"g_out_b{b}_", 1, [P, GT, D], F32)
        h_ring = core.ring(ctx, f"h_b{b}_", 2, [P, GROUP], F32)
        h_hi = core.ring(ctx, f"h_hi_b{b}_", 2, [P, GROUP], F32R)
        h_lo = core.ring(ctx, f"h_lo_b{b}_", 2, [P, GROUP], F32R)
        norm = LayerNorm(core, ctx, consts, f"ln0_b{b}", 1)

        def load_group(g):
            xs = x_ring.take()
            rows = x_dram[(b * GROUPS + g) * GROUP:(b * GROUPS + g + 1) * GROUP, :]
            loaded = core.sp.dma(xs.dma_sem, lambda e: e.dma_start(
                xs.view[:, :, :], rows.rearrange("(j p) d -> p j d", p=P)), *xs.free)
            tiles = [xs.view[:, j, :] for j in range(GT)]
            yield
            normed = norm(tiles, tiles, GT, loaded)
            hi, lo, half = xt_hi.take(), xt_lo.take(), xt_16.take()
            freed = []
            for c in range(DC):
                yield
                bank = tr_ring.take()
                for j in range(GT):
                    done = core.pe.do(lambda e, j=j, c=c, bank=bank: e.transpose(
                        bank.view[:, j * P:(j + 1) * P], xs.view[:, j, c * P:(c + 1) * P], consts.identity[:, :]),
                        normed, *bank.free, signal=(j == GT - 1))
                freed.append(done)
                if c == 0:
                    done = core.act.do(lambda e, bank=bank: e.activation(half.view[:, :], bank.view, ACT.Copy),
                                       done, *half.free)
                split = split_from_psum(core, bank.view, hi.view[:, c, :], lo.view[:, c, :], done, *hi.free)
                bank.free = [split]
            xs.free = freed
            return hi, lo, half, split

        def group(g, ready):
            hi, lo, half, split = ready

            def qk_block(col):
                bank = mm_ring.take()
                cols = slice(col, col + P)
                core.pe.do(lambda e: e.matmul(bank.view, w.qkv_16[:, cols], half.view[:, :], start=True, stop=False),
                           split, w.ready, *bank.free, signal=False)
                core.pe.do(lambda e: e.matmul(bank.view, w.qkv_hi[:, cols], hi.view[:, 1, :], start=False, stop=False), signal=False)
                core.pe.do(lambda e: e.matmul(bank.view, w.qkv_hi[:, cols], lo.view[:, 1, :], start=False, stop=False), signal=False)
                done = core.pe.do(lambda e: e.matmul(bank.view, w.qkv_lo[:, cols], hi.view[:, 1, :], start=False, stop=True))
                return bank, done

            q_out = q_ring.take()
            for m in range(DC):
                bank, done = qk_block(m * P)
                sent = core.act.do(lambda e, m=m, bank=bank: e.activation(
                    q_out.view[:, m, :], bank.view, ACT.Copy, scale=float(D) ** -0.5), done, *q_out.free)
                bank.free = [sent]
            q_out.free = [core.sp.dma(q_out.dma_sem, lambda e: e.dma_start(q_dram[b * GROUPS + g], q_out.view[:, :, :]), sent)]
            yield
            for m in range(DC):
                bank, done = qk_block(D + m * P)
                cols = slice(g * GROUP, (g + 1) * GROUP)
                bank.free = [split_from_psum(core, bank.view, kv.k_hi[:, m, cols], kv.k_lo[:, m, cols], done)]
            yield
            for pair in range(GT // 2):
                bank = mm_ring.take()
                for half_bank in range(2):
                    j = 2 * pair + half_bank
                    rows = slice(j * P, (j + 1) * P)
                    out = bank.view[:, half_bank * D:(half_bank + 1) * D]
                    core.pe.do(lambda e, rows=rows, out=out: e.matmul(out, half.view[:, rows], w.qkv_16[:, 2 * D:3 * D], start=True, stop=False),
                               *bank.free, signal=False)
                    core.pe.do(lambda e, rows=rows, out=out: e.matmul(out, hi.view[:, 1, rows], w.qkv_hi[:, 2 * D:3 * D], start=False, stop=False), signal=False)
                    core.pe.do(lambda e, rows=rows, out=out: e.matmul(out, hi.view[:, 1, rows], w.qkv_lo[:, 2 * D:3 * D], start=False, stop=False), signal=False)
                    done = core.pe.do(lambda e, rows=rows, out=out: e.matmul(out, lo.view[:, 1, rows], w.qkv_hi[:, 2 * D:3 * D], start=False, stop=True),
                                      signal=(half_bank == 1))
                blocks = slice(g * GT + 2 * pair, g * GT + 2 * pair + 2)
                psum = bank.view.rearrange("p (t d) -> p t d", t=2)
                bank.free = [split_from_psum(core, psum, kv.v[:, blocks, 0:D], kv.v[:, blocks, D:2 * D], done)]
            half.free = [done]
            for f in range(w.hidden_blocks + 1):
                yield
                if f < w.hidden_blocks:
                    bank = hid_ring.take()
                    for c in range(DC):
                        for part in (hi, lo):
                            last = c == DC - 1 and part is lo
                            done = core.pe.do(lambda e, f=f, c=c, part=part, bank=bank, last=last: e.matmul(
                                bank.view, w.sign1[:, c, f * P:(f + 1) * P], part.view[:, c, :],
                                start=(c == 0 and part is hi), stop=last), *bank.free, signal=last)
                    h, hh, hl = h_ring.take(), h_hi.take(), h_lo.take()
                    a = core.act.do(lambda e, f=f, bank=bank, hh=hh: e.activation(
                        hh.view[:, :], bank.view, ACT.Gelu, bias=w.b1[:, f:f + 1], scale=w.alpha1[:, f:f + 1]),
                        done, *hh.free)
                    a = core.act.do(lambda e, f=f, bank=bank, h=h: e.activation(
                        h.view[:, :], bank.view, ACT.Gelu, bias=w.b1[:, f:f + 1], scale=w.alpha1[:, f:f + 1]),
                        *h.free)
                    bank.free = [a]
                    l = core.dve.do(lambda e, h=h, hh=hh, hl=hl: e.tensor_tensor(
                        hl.view[:, :], h.view[:, :], f32(hh.view[:, :]), ALU.subtract), a, *hh.free)
                    h.free = [l]
                    this = (hh, hl, l)
                    if f == w.hidden_blocks - 1:
                        hi.free = [done]
                if f > 0:
                    hh, hl, ready_h = before
                    for j in range(GT):
                        ob = out_banks[j // 2]
                        out = ob.view[:, (j % 2) * D:(j % 2 + 1) * D]
                        for part in (hh, hl):
                            first = f == 1 and part is hh and j % 2 == 0
                            last = f == w.hidden_blocks and part is hl
                            done = core.pe.do(lambda e, j=j, f=f, part=part, out=out, first=first, last=last: e.matmul(
                                out, part.view[:, j * P:(j + 1) * P], w.sign2[:, f - 1, :],
                                start=first, stop=last, skip_group_check=True),
                                ready_h, *(ob.free if f == 1 else []), signal=(j == GT - 1 and part is hl))
                    hh.free = [done]
                if f < w.hidden_blocks:
                    before = this
            g_out = g_ring.take()
            for half_bank, ob in enumerate(out_banks):
                view = g_out.view[:, 2 * half_bank:2 * half_bank + 2, :]
                psum = ob.view.rearrange("p (t d) -> p t d", t=2)
                t = core.dve.do(lambda e, view=view, psum=psum: e.tensor_tensor(
                    view, psum, w.alpha2[:, :].unsqueeze(1).broadcast_to([P, 2, D]), ALU.mult), done, *g_out.free)
                ob.free = [t]
                sent = core.dve.do(lambda e, view=view: e.tensor_tensor(
                    view, view, w.b2[:, :].unsqueeze(1).broadcast_to([P, 2, D]), ALU.add), t)
            rows = g_dram[(b * GROUPS + g) * GROUP:(b * GROUPS + g + 1) * GROUP, :]
            g_out.free = [core.sp.dma(g_out.dma_sem, lambda e: e.dma_start(
                rows.rearrange("(j p) d -> p j d", p=P), g_out.view[:, :, :]), sent)]

        ready = finish(load_group(0))
        for g in range(GROUPS):
            ahead = load_group(g + 1) if g + 1 < GROUPS else None
            ready = merge(group(g, ready), ahead)
        core.hand_over()


def finish(thread):
    while True:
        try:
            next(thread)
        except StopIteration as e:
            return e.value


def merge(main, ahead):
    result = None
    for _ in main:
        if ahead is not None:
            try:
                next(ahead)
            except StopIteration as e:
                result, ahead = e.value, None
    if ahead is not None:
        result = finish(ahead)
    return result


class Layer0Weights:

    def __init__(self, core, ctx, consts, a):
        self.hidden_blocks = a["w1T"].shape[1] // P
        hb = self.hidden_blocks
        hidden = hb * P
        self.qkv_16 = core.sb(ctx, "qkv_16", [P, 3 * D], F16)
        self.qkv_hi = core.sb(ctx, "qkv_hi", [P, 3 * D], F32R)
        self.qkv_lo = core.sb(ctx, "qkv_lo", [P, 3 * D], F32R)
        self.sign1 = core.sb(ctx, "sign1", [P, DC, hidden], F32R)
        self.sign2 = core.sb(ctx, "sign2", [P, hb, D], F32R)
        self.alpha1 = core.sb(ctx, "alpha1", [P, hb], F32)
        self.b1 = core.sb(ctx, "b1", [P, hb], F32)
        self.alpha2 = core.sb(ctx, "alpha2", [P, D], F32)
        self.b2 = core.sb(ctx, "b2", [P, D], F32)
        self.wo_hi = core.sb(ctx, "wo_hi", [P, DC, D], F32R)
        self.wo_lo = core.sb(ctx, "wo_lo", [P, DC, D], F32R)
        self.out_b = core.sb(ctx, "out_b", [P, D], F32)
        vecs = DmaSem(core, "layer0_vectors_dma")
        core.sp.dma(vecs, lambda e: e.dma_start(self.b1[:, :], a["b1"].rearrange("(f p) -> p f", p=P), allow_slow_non_contiguous=True))
        core.sp.dma(vecs, lambda e: e.dma_start(self.b2[:, :], a["b2"].partition_broadcast(P)))
        loaded = core.sp.dma(vecs, lambda e: e.dma_start(self.out_b[:, :], a["out_b"].partition_broadcast(P)))
        with ExitStack() as tmp:
            bank = tmp.enter_context(core.nc.psum_tensor("alpha2_bank", [P, BANK], F32))
            stage = core.dma_ring(tmp, "layer0_stage", 4, [P, 2048], F32)
            mask = core.sb(tmp, "negative", [P, 2048], F32)
            alpha2_col = core.sb(tmp, "alpha2_col", [P, DC], F32)
            alpha2_wide = core.sb(tmp, "alpha2_wide", [P, DC, P], F32)
            dve = core.dve

            def load(dram, shape):
                s = stage.take()
                n = shape[0] * shape[1]
                view = s.view[:, 0:n].rearrange("p (a n) -> p a n", a=shape[0])
                return s, view, core.sp.dma(s.dma_sem, lambda e: e.dma_start(view, dram), *s.free)

            s, v, t = load(a["qkv"].rearrange("(c p) n -> p c n", p=P), (DC, 3 * D))
            dve.do(lambda e, v=v: e.tensor_copy(self.qkv_16[:, :], v[:, 0, :]), t)
            s.free = [split_weights(core, v[:, 1, :], self.qkv_hi[:, :], self.qkv_lo[:, :], t)]
            s, v, t = load(a["w1"].rearrange("(f p) d -> p f d", p=P), (hb, D))
            u = dve.do(lambda e, v=v: e.tensor_reduce(self.alpha1[:, :], v, AX_X, ALU.add, apply_absolute_value=True), t)
            s.free = [u]
            dve.do(lambda e: e.tensor_scalar(self.alpha1[:, :], self.alpha1[:, :], 1.0 / D, None, ALU.mult), u)
            s, v, t = load(a["w2"].rearrange("(c p) h -> p c h", p=P), (DC, hidden))
            u = dve.do(lambda e, v=v: e.tensor_reduce(alpha2_col[:, :], v, AX_X, ALU.add, apply_absolute_value=True), t)
            s.free = [u]
            for c in range(DC):
                u2 = dve.do(lambda e, c=c: e.tensor_scalar(
                    alpha2_wide[:, c, :], consts.ones[:, :], alpha2_col[:, c:c + 1], 1.0 / hidden, ALU.mult, ALU.mult),
                    u, consts.ready)
            for c in range(DC):
                m = core.pe.do(lambda e, c=c: e.matmul(bank[:, c * P:(c + 1) * P], alpha2_wide[:, c, :], consts.identity[:, :],
                                                       start=True, stop=True), u2, consts.ready)
            dve.do(lambda e: e.tensor_copy(self.alpha2[:, :], bank[:, 0:D]), m)
            masked = None
            for dram, shape, out in (
                (a["w1T"].rearrange("(c p) h -> p c h", p=P), (DC, hidden), self.sign1),
                (a["w2T"].rearrange("(f p) d -> p f d", p=P), (hb, D), self.sign2),
            ):
                s, v, t = load(dram, shape)
                m = mask[:, 0:shape[0] * shape[1]].rearrange("p (a n) -> p a n", a=shape[0])
                u = dve.do(lambda e, v=v, m=m: e.tensor_scalar(m, v, 0.0, None, ALU.is_lt), t, masked)
                masked = dve.do(lambda e, v=v, m=m, out=out: e.scalar_tensor_tensor(
                    out[:, :, :], v, 0.0, m, ALU.is_gt, ALU.subtract), u)
                s.free = [masked]
            s, v, t = load(a["woT"].rearrange("(c p) n -> p c n", p=P), (DC, D))
            self.ready = split_weights(core, v, self.wo_hi[:, :, :], self.wo_lo[:, :, :], t, loaded)
            s.free = [self.ready]
            core.hand_over()


class KeysValues:

    def __init__(self, core, ctx):
        self.k_hi = core.sb(ctx, "k_hi", [P, DC, SEQ], F32R)
        self.k_lo = core.sb(ctx, "k_lo", [P, DC, SEQ], F32R)
        self.v = core.sb(ctx, "v_hi_lo", [P, SEQ // P, 2 * D], F32R)


KEYS = 1024
KEY_CHUNKS = SEQ // KEYS
KEY_BLOCKS = KEYS // P


def attention(core, consts, w, kv, b, x_dram, q_dram, g_dram, x1_dram, xn1_dram):
    pe, act, dve, pool, sp = core.lanes
    with ExitStack() as ctx:
        banks_s = [ctx.enter_context(core.nc.psum_tensor(f"scores{b}_{i}", [P, KEYS], F32)) for i in range(2)]
        s_ring = Ring([Slot(t) for t in banks_s])
        pt_ring = Ring([Slot(ctx.enter_context(core.nc.psum_tensor(f"pt{b}_{i}", [P, BANK], F32))) for i in range(2)])
        y_bank = Slot(ctx.enter_context(core.nc.psum_tensor(f"ybank{b}", [P, 2 * D], F32)))
        misc = Slot(ctx.enter_context(core.nc.psum_tensor(f"misc{b}", [P, BANK], F32)))
        q_raw = core.dma_ring(ctx, f"q_raw_b{b}_", 1, [P, DC, GROUP], F32)
        q_hi = core.ring(ctx, f"q_hi_b{b}_", 2, [P, DC, GROUP], F32R)
        q_lo = core.ring(ctx, f"q_lo_b{b}_", 2, [P, DC, GROUP], F32R)
        p_ring = core.ring(ctx, f"p_b{b}_", 2, [P, KEYS], F32)
        pt_hi = core.ring(ctx, f"pt_hi_b{b}_", 2, [P, BANK], F32R)
        pt_lo = core.ring(ctx, f"pt_lo_b{b}_", 2, [P, BANK], F32R)
        acc_ring = core.ring(ctx, f"acc_b{b}_", 2, [P, D], F32)
        col_ring = core.ring(ctx, f"softmax_cols_b{b}_", 2, [P, 5, KEY_CHUNKS + 1], F32)
        yt_hi = core.sb(ctx, f"yt_hi_b{b}", [P, DC, P], F32R)
        yt_lo = core.sb(ctx, f"yt_lo_b{b}", [P, DC, P], F32R)
        x_ring = core.dma_ring(ctx, f"x_res_b{b}_", 2, [P, D], F32)
        g_ring = core.dma_ring(ctx, f"g_in_b{b}_", 2, [P, D], F32)
        e_ring = core.ring(ctx, f"gate_b{b}_", 1, [P, D], F32)
        xn_ring = core.dma_ring(ctx, f"xn1_out_b{b}_", 1, [P, D], F32)
        norm = LayerNorm(core, ctx, consts, f"ln1_b{b}", 1)
        tiles = SEQ // P
        steps = [(t, c) for t in range(tiles) for c in range(KEY_CHUNKS)]
        state = {}
        yt_free = [None]

        def queries(group):
            raw, hi, lo = q_raw.take(), q_hi.take(), q_lo.take()
            t = sp.dma(raw.dma_sem, lambda e: e.dma_start(raw.view[:, :, :], q_dram[b * GROUPS + group]), *raw.free)
            th = dve.do(lambda e: e.tensor_copy(hi.view[:, :, :], raw.view[:, :, :]), t, *hi.free)
            tl = dve.do(lambda e: e.tensor_tensor(lo.view[:, :, :], raw.view[:, :, :], f32(hi.view[:, :, :]), ALU.subtract), th)
            raw.free = [tl]
            return hi, lo, tl

        def scores(i, half):
            t, c = steps[i]
            if half == 0:
                slot = s_ring.take()
                state[i] = {"s": slot}
            slot = state[i]["s"]
            hi, lo, ready = state["q", t // GT]
            rows = slice((t % GT) * P, (t % GT + 1) * P)
            keys = slice(c * KEYS + half * BANK, c * KEYS + (half + 1) * BANK)
            out = slot.view[:, half * BANK:(half + 1) * BANK]
            for n, (d, qs, ks) in enumerate([(d, qs, ks) for d in range(DC) for qs, ks in ((hi, kv.k_hi), (hi, kv.k_lo), (lo, kv.k_hi))]):
                done = pe.do(lambda e, n=n, d=d, qs=qs, ks=ks: e.matmul(out, qs.view[:, d, rows], ks[:, d, keys],
                                                                       start=(n == 0), stop=(n == 3 * DC - 1)),
                             ready, *slot.free, signal=(n == 3 * DC - 1))
            state[i]["scored"] = done
            if c == KEY_CHUNKS - 1 and half == 1 and t % GT == GT - 1:
                hi.free = [done]

        def running_max(i):
            t, c = steps[i]
            st = state[i]
            if c == 0:
                state["cols", t] = col_ring.take()
            cols = state["cols", t]
            v = cols.view
            free = cols.free if c == 0 else []
            slot = st["s"]
            m = dve.do(lambda e: e.tensor_reduce(v[:, 0, c:c + 1], slot.view[:, :], AX_X, ALU.max, negate=True), st["scored"], *free)
            if c == 0:
                m = dve.do(lambda e: e.tensor_copy(v[:, 1, 0:1], v[:, 0, 0:1]), m)
            else:
                m = dve.do(lambda e: e.tensor_tensor(v[:, 1, c:c + 1], v[:, 1, c - 1:c], v[:, 0, c:c + 1], ALU.min), m)
            st["max"] = m

        def exponentials(i):
            t, c = steps[i]
            st = state[i]
            v = state["cols", t].view
            p = p_ring.take()
            st["p"] = p
            slot = st["s"]
            st["exp"] = act.do(lambda e: e.activation(p.view[:, :], slot.view[:, :], ACT.Exp, bias=v[:, 1, c:c + 1],
                                                      accum_out=v[:, 3, c:c + 1]), st["max"], *p.free)
            slot.free = [st["exp"]]
            if c:
                st["corr"] = act.do(lambda e: e.activation(v[:, 2, c:c + 1], v[:, 1, c - 1:c], ACT.Exp, bias=v[:, 1, c:c + 1], scale=-1.0))

        def turn(i, half):
            st = state[i]
            bank, hi, lo = pt_ring.take(), pt_hi.take(), pt_lo.take()
            for k in range(4):
                kb = 4 * half + k
                done = pe.do(lambda e, k=k, kb=kb: e.transpose(bank.view[:, k * P:(k + 1) * P], st["p"].view[:, kb * P:(kb + 1) * P],
                                                               consts.identity[:, :]), st["exp"], *bank.free, signal=(k == 3))
            if half == 1:
                st["p"].free = [done]
            th = act.do(lambda e: e.activation(hi.view[:, :], bank.view[:, :], ACT.Copy), done, *hi.free)
            tl = dve.do(lambda e: e.tensor_tensor(lo.view[:, :], bank.view[:, :], f32(hi.view[:, :]), ALU.subtract), th, *hi.free)
            bank.free = [tl]
            st["pt", half] = (hi, lo, tl)

        def values(i, half):
            t, c = steps[i]
            st = state[i]
            hi, lo, ready = st["pt", half]
            for k in range(4):
                kb = 4 * half + k
                block = c * KEY_BLOCKS + kb
                pe.do(lambda e, k=k, kb=kb, block=block: e.matmul(y_bank.view[:, :], hi.view[:, k * P:(k + 1) * P], kv.v[:, block, :],
                                                                  start=(kb == 0), stop=False, skip_group_check=True),
                      ready, *y_bank.free, signal=False)
                done = pe.do(lambda e, k=k, kb=kb, block=block: e.matmul(y_bank.view[:, 0:D], lo.view[:, k * P:(k + 1) * P], kv.v[:, block, 0:D],
                                                                        start=False, stop=(kb == KEY_BLOCKS - 1), skip_group_check=True),
                             signal=(k == 3))
            hi.free = [done]
            st["pv"] = done

        def accumulate(i):
            t, c = steps[i]
            st = state[i]
            v = state["cols", t].view
            if c == 0:
                state["acc", t] = acc_ring.take()
                acc = state["acc", t]
                a = dve.do(lambda e: e.tensor_copy(acc.view[:, :], y_bank.view[:, 0:D]), st["pv"], *acc.free)
                l = dve.do(lambda e: e.tensor_copy(v[:, 4, 0:1], v[:, 3, 0:1]), st["exp"])
            else:
                acc = state["acc", t]
                a = dve.do(lambda e: e.scalar_tensor_tensor(acc.view[:, :], acc.view[:, :], v[:, 2, c:c + 1], y_bank.view[:, 0:D],
                                                            ALU.mult, ALU.add), st["pv"], st["corr"], state["acc_done", t])
                l = dve.do(lambda e: e.scalar_tensor_tensor(v[:, 4, c:c + 1], v[:, 4, c - 1:c], v[:, 2, c:c + 1], v[:, 3, c:c + 1],
                                                            ALU.mult, ALU.add), state["sum_done", t])
            a = dve.do(lambda e: e.tensor_tensor(acc.view[:, :], acc.view[:, :], y_bank.view[:, D:2 * D], ALU.add), a)
            y_bank.free = [a]
            state["acc_done", t], state["sum_done", t] = a, l

        def residual(t):
            acc, cols = state["acc", t], state["cols", t]
            v = cols.view
            row = (b * SEQ + t * P, b * SEQ + (t + 1) * P)
            xs, gs, es = x_ring.take(), g_ring.take(), e_ring.take()
            x_in = sp.dma(xs.dma_sem, lambda e: e.dma_start(xs.view[:, :], x_dram[row[0]:row[1], :]), *xs.free)
            g_in = sp.dma(gs.dma_sem, lambda e: e.dma_start(gs.view[:, :], g_dram[row[0]:row[1], :]), *gs.free)
            te = act.do(lambda e: e.activation(es.view[:, :], gs.view[:, :], ACT.Exp, scale=-1.0), g_in, *es.free)
            te = pool.do(lambda e: e.tensor_scalar(es.view[:, :], es.view[:, :], 1.0, 1.0, ALU.mult, ALU.add), te)
            te = dve.do(lambda e: e.reciprocal(es.view[:, :], es.view[:, :]), te)
            te = pool.do(lambda e: e.tensor_tensor(es.view[:, :], es.view[:, :], gs.view[:, :], ALU.mult), te)
            gs.free = [te]
            tr = dve.do(lambda e: e.reciprocal(v[:, 0, KEY_CHUNKS:KEY_CHUNKS + 1], v[:, 4, KEY_CHUNKS - 1:KEY_CHUNKS]), state["sum_done", t])
            ty = dve.do(lambda e: e.tensor_scalar(acc.view[:, :], acc.view[:, :], v[:, 0, KEY_CHUNKS:KEY_CHUNKS + 1], None, ALU.mult), tr)
            cols.free = [ty]
            yield
            for c in range(DC):
                done = pe.do(lambda e, c=c: e.transpose(misc.view[:, c * P:(c + 1) * P], acc.view[:, c * P:(c + 1) * P], consts.identity[:, :]),
                             ty, *misc.free, signal=(c == DC - 1))
            acc.free = [done]
            pair = misc.view[:, 0:D].rearrange("p (c q) -> p c q", c=DC)
            split = split_from_psum(core, pair, yt_hi[:, :, :], yt_lo[:, :, :], done, yt_free[0])
            yield
            out = misc.view[:, D:2 * D]
            for n, (c, ys, ws) in enumerate([(c, ys, ws) for c in range(DC) for ys, ws in ((yt_hi, w.wo_hi), (yt_hi, w.wo_lo), (yt_lo, w.wo_hi))]):
                done = pe.do(lambda e, n=n, c=c, ys=ys, ws=ws: e.matmul(out, ys[:, c, :], ws[:, c, :], start=(n == 0), stop=(n == 3 * DC - 1)),
                             split, signal=(n == 3 * DC - 1))
            yt_free[0] = done
            ts = dve.do(lambda e: e.tensor_tensor(acc.view[:, :], out, w.out_b[:, :], ALU.add), done)
            misc.free = [ts]
            ts = pool.do(lambda e: e.tensor_tensor(acc.view[:, :], acc.view[:, :], es.view[:, :], ALU.mult), ts, te)
            es.free = [ts]
            ts = pool.do(lambda e: e.tensor_tensor(xs.view[:, :], xs.view[:, :], acc.view[:, :], ALU.add), ts, x_in)
            acc.free = [ts]
            saved = sp.dma(xs.dma_sem, lambda e: e.dma_start(x1_dram[row[0]:row[1], :], xs.view[:, :]), ts)
            yield
            xn = xn_ring.take()
            tn = norm([xs.view[:, :]], [xn.view[:, :]], 1, ts, *xn.free)
            xs.free = [saved, tn]
            xn.free = [sp.dma(xn.dma_sem, lambda e: e.dma_start(xn1_dram[row[0]:row[1], :], xn.view[:, :]), tn)]

        state["q", 0] = queries(0)
        scores(0, 0)
        scores(0, 1)
        running_max(0)
        exponentials(0)
        pending = None
        for i, (t, c) in enumerate(steps):
            more = i + 1 < len(steps)
            if c == 1 and t % GT == 2 and t // GT + 1 < tiles // GT:
                state["q", t // GT + 1] = queries(t // GT + 1)
            if more:
                scores(i + 1, 0)
            turn(i, 0)
            if more:
                scores(i + 1, 1)
                running_max(i + 1)
            turn(i, 1)
            if more:
                exponentials(i + 1)
            values(i, 0)
            if pending is not None:
                next(pending, None)
            values(i, 1)
            accumulate(i)
            state.pop(i)
            if c == KEY_CHUNKS - 1:
                if pending is not None:
                    finish(pending)
                pending = residual(t)
        finish(pending)
        core.hand_over()
CHUNK = 512
CHUNKS = SEQ // CHUNK
INNER = 128
STATES = 64
EXPERTS = 16
CAPACITY = 2 * SEQ // EXPERTS
LISTS = BATCH * EXPERTS
TILES = SEQ // P
SLOT_TILES = CAPACITY // P
HIDDEN = 512
HB = HIDDEN // P
ROWS16, COLS32 = 16, 32
SCORE_BITS = 30


class ScanWeights:
    def __init__(self, core, ctx, consts, a):
        sb = core.sb
        self.up_hi = sb(ctx, "up_hi", [P, DC, D], F32R)
        self.up_lo = sb(ctx, "up_lo", [P, DC, D], F32R)
        self.delta_hi = sb(ctx, "wdelta_hi", [P, INNER], F32R)
        self.delta_lo = sb(ctx, "wdelta_lo", [P, INNER], F32R)
        self.bc_hi = sb(ctx, "bc_hi", [P, 2, P], F32R)
        self.bc_lo = sb(ctx, "bc_lo", [P, 2, P], F32R)
        self.down_hi = sb(ctx, "down_hi", [P, D], F32R)
        self.down_lo = sb(ctx, "down_lo", [P, D], F32R)
        self.b_down = sb(ctx, "b_down", [P, D], F32)
        self.gamma = sb(ctx, "gamma", [P, DC], F32)
        self.beta = sb(ctx, "beta", [P, DC], F32)
        self.b_up = sb(ctx, "b_up", [P, DC], F32)
        self.conv_w = sb(ctx, "conv_w", [P, 3], F32)
        self.conv_b = sb(ctx, "conv_b", [P, 1], F32)
        self.b_delta = sb(ctx, "b_delta", [P, 1], F32)
        self.skip = sb(ctx, "skip", [P, 1], F32)
        self.a = sb(ctx, "a_neg", [P, STATES], F32)
        self.select = sb(ctx, "select_state", [P, STATES], F32R)
        vecs = DmaSem(core, "scan_vectors_dma")
        col = lambda ap: ap.rearrange("(c p) -> p c", p=P)
        for dst, src in ((self.gamma, col(a["ln_gamma"])), (self.beta, col(a["ln_beta"])), (self.b_up, col(a["b_up"])),
                         (self.conv_w, a["conv_w"]), (self.conv_b, col(a["conv_b"])), (self.b_delta, col(a["b_delta"])),
                         (self.skip, col(a["D"])), (self.a, a["A_log"]), (self.b_down, a["b_down"].partition_broadcast(P))):
            vt = core.sp.dma(vecs, lambda e, dst=dst, src=src: e.dma_start(dst[:, :], src, allow_slow_non_contiguous=True))
        t = core.act.do(lambda e: e.activation(self.a[:, :], self.a[:, :], ACT.Exp), vt)
        core.dve.do(lambda e: e.tensor_scalar(self.a[:, :], self.a[:, :], -1.0, None, ALU.mult), t)
        with ExitStack() as tmp:
            stage = DmaSem(core, "scan_stage_dma")
            up = core.sb(tmp, "up_raw", [P, DC, D], F32)
            delta = core.sb(tmp, "wdelta_raw", [P, INNER], F32)
            bc = core.sb(tmp, "bc_raw", [P, 2, 2, STATES], F32)
            down = core.sb(tmp, "down_raw", [P, D], F32)
            sel = core.sb(tmp, "select_raw", [P, STATES], F32)
            core.sp.dma(stage, lambda e: e.dma_start(up[:, :, :], a["W_up"].rearrange("(c p) n -> p c n", p=P)))
            core.sp.dma(stage, lambda e: e.dma_start(delta[:, :], a["W_delta"]))
            for m, name in enumerate(("W_B", "W_C")):
                for twice in range(2):
                    core.sp.dma(stage, lambda e, m=m, name=name, twice=twice: e.dma_start(bc[:, m, twice, :], a[name]))
            t = core.sp.dma(stage, lambda e: e.dma_start(down[:, :], a["W_down"]))
            split_weights(core, up[:, :, :], self.up_hi[:, :, :], self.up_lo[:, :, :], t)
            split_weights(core, delta[:, :], self.delta_hi[:, :], self.delta_lo[:, :])
            split_weights(core, bc[:, :, :, :].rearrange("p m t n -> p m (t n)"), self.bc_hi[:, :, :], self.bc_lo[:, :, :])
            split_weights(core, down[:, :], self.down_hi[:, :], self.down_lo[:, :])
            t = core.pool.do(lambda e: e.memset(sel[:, :], 0.0))
            for half in range(2):
                t = core.pool.do(lambda e, half=half: e.affine_select(
                    out=sel[:, :], in_=sel[:, :], compare_op=ALU.not_equal, fill=1.0,
                    base=-STATES * half, pattern=[[-1, STATES]], channel_multiplier=1), t)
            core.dve.do(lambda e: e.tensor_copy(self.select[:, :], sel[:, :]), t)
            core.hand_over()


class SelectiveScan:

    def __init__(self, core, ctx, consts, w, banks, a, xn_dram, s_dram):
        self.core, self.consts, self.w, self.xn_dram, self.s_dram = core, consts, w, xn_dram, s_dram
        ring = lambda name, n, shape=(P, CHUNK), dt=F32: core.ring(ctx, name, n, list(shape), dt)
        self.b_banks = Ring([Slot(banks[0][:, :]), Slot(banks[1][:, :])])
        self.c_banks = Ring([Slot(banks[2][:, :]), Slot(banks[3][:, :])])
        self.y_bank = Slot(banks[4][:, :])
        self.bank = Slot(banks[5][:, :])
        self.xn = core.dma_ring(ctx, "scan_xn", 2, [P, GT, D], F32)
        self.yn = ring("scan_yn", 1, (P, GT, D))
        self.yt = ring("scan_yt", 1)
        self.yt_hi = core.sb(ctx, "scan_yt_hi", [P, DC, CHUNK], F32R)
        self.yt_lo = core.sb(ctx, "scan_yt_lo", [P, DC, CHUNK], F32R)
        self.yt_free = None
        self.left = core.sb(ctx, "scan_left", [P, 2 + CHUNK], F32)
        self.left_free = None
        self.gate = ring("scan_gate", 2)
        self.temp = ring("scan_temp", 4)
        self.u = ring("scan_u", 2)
        self.u_hi = ring("scan_u_hi", 1, dt=F32R)
        self.u_lo = ring("scan_u_lo", 1, dt=F32R)
        self.delta = ring("scan_delta", 2)
        self.du = ring("scan_du", 2)
        self.bb = ring("scan_bb", 2, dt=F32R)
        self.cc = ring("scan_cc", 2, dt=F32R)
        self.out = core.dma_ring(ctx, "scan_out", 1, [P, 2, D], F32)
        self.decay = ring("scan_decay", 4)
        self.drive = ring("scan_drive", 2)
        self.h = ring("scan_h", 2)
        self.ch = ring("scan_ch", 3)
        self.state = core.sb(ctx, "scan_state", [P, STATES], F32)
        self.state_free = {}
        self.norm = LayerNorm(core, ctx, consts, "ln_scan", 1)

    def silu(self, x, out, ready, *free):
        core = self.core
        e = self.temp.take()
        t = core.act.do(lambda g: g.activation(e.view[:, :], x, ACT.Exp, scale=-1.0), ready, *e.free)
        t = core.pool.do(lambda g: g.tensor_scalar(e.view[:, :], e.view[:, :], 1.0, 1.0, ALU.mult, ALU.add), t)
        t = core.dve.do(lambda g: g.reciprocal(e.view[:, :], e.view[:, :]), t)
        t = core.pool.do(lambda g: g.tensor_tensor(out, x, e.view[:, :], ALU.mult), t, *free)
        e.free = [t]
        return t

    def prepare(self, chunk):
        core, w, consts = self.core, self.w, self.consts
        pe, act, dve, pool, sp = core.lanes
        st = {}
        xs, yn = self.xn.take(), self.yn.take()
        rows = self.xn_dram[chunk * CHUNK:(chunk + 1) * CHUNK, :]
        loaded = sp.dma(xs.dma_sem, lambda e: e.dma_start(xs.view[:, :, :], rows.rearrange("(j p) d -> p j d", p=P)), *xs.free)
        st["xn"], st["loaded"] = xs, loaded
        yield
        normed = self.norm([xs.view[:, j, :] for j in range(GT)], [yn.view[:, j, :] for j in range(GT)], GT, loaded, *yn.free)
        bank = self.bank
        for c in range(DC):
            yield
            for j in range(GT):
                done = pe.do(lambda e, j=j, c=c: e.transpose(bank.view[:, j * P:(j + 1) * P], yn.view[:, j, c * P:(c + 1) * P], consts.identity[:, :]),
                             normed, *bank.free, signal=(j == GT - 1))
            yt = self.yt.take()
            t = act.do(lambda e, c=c: e.activation(yt.view[:, :], bank.view, ACT.Identity, bias=w.beta[:, c:c + 1], scale=w.gamma[:, c:c + 1]),
                       done, *yt.free)
            bank.free = [t]
            split = split_weights_on_pool(core, yt.view[:, :], self.yt_hi[:, c, :], self.yt_lo[:, c, :], t, self.yt_free)
            yt.free = [split]
        yn.free = [done]

        def project(cols):
            parts = [(c, ws, ys) for c in range(DC) for ws, ys in ((w.up_hi, self.yt_hi), (w.up_hi, self.yt_lo), (w.up_lo, self.yt_hi))]
            for n, (c, ws, ys) in enumerate(parts):
                done = pe.do(lambda e, n=n, c=c, ws=ws, ys=ys: e.matmul(bank.view, ws[:, c, cols], ys[:, c, :], start=(n == 0), stop=(n == len(parts) - 1)),
                             split, *bank.free, signal=(n == len(parts) - 1))
            return done

        yield
        if chunk % CHUNKS == 0:
            t = dve.do(lambda e: e.memset(self.left[:, 0:2], 0.0), self.left_free)
        else:
            t = dve.do(lambda e: e.tensor_copy(self.left[:, 0:2], self.left[:, CHUNK:CHUNK + 2]), self.left_free)
        done = project(slice(0, INNER))
        left_in = act.do(lambda e: e.activation(self.left[:, 2:2 + CHUNK], bank.view, ACT.Identity, bias=w.b_up[:, 0:1]), done, t)
        bank.free = [left_in]
        yield
        done = project(slice(INNER, 2 * INNER))
        self.yt_free = done
        right, gate = self.temp.take(), self.gate.take()
        t = act.do(lambda e: e.activation(right.view[:, :], bank.view, ACT.Identity, bias=w.b_up[:, 1:2]), done, *right.free)
        bank.free = [t]
        t = self.silu(right.view[:, :], gate.view[:, :], t, *gate.free)
        right.free = [t]
        st["gate"], st["gate_ready"] = gate, t
        yield
        conv = self.temp.take()
        t = dve.do(lambda e: e.tensor_scalar(conv.view[:, :], self.left[:, 0:CHUNK], w.conv_w[:, 0:1], w.conv_b[:, 0:1], ALU.mult, ALU.add),
                   left_in, *conv.free)
        for k in (1, 2):
            t = dve.do(lambda e, k=k: e.scalar_tensor_tensor(conv.view[:, :], self.left[:, k:k + CHUNK], w.conv_w[:, k:k + 1], conv.view[:, :],
                                                             ALU.mult, ALU.add), t)
        self.left_free = t
        u, u_hi, u_lo = self.u.take(), self.u_hi.take(), self.u_lo.take()
        t = self.silu(conv.view[:, :], u.view[:, :], t, *u.free)
        conv.free = [t]
        st["u"], u_ready = u, t
        split = split_weights_on_pool(core, u.view[:, :], u_hi.view[:, :], u_lo.view[:, :], t, *u_hi.free)
        yield

        def from_u(hi, lo):
            for n, (ws, us) in enumerate(((hi, u_hi), (hi, u_lo), (lo, u_hi))):
                done = pe.do(lambda e, n=n, ws=ws, us=us: e.matmul(bank.view, ws, us.view[:, :], start=(n == 0), stop=(n == 2)),
                             split, *bank.free, signal=(n == 2))
            return done

        done = from_u(w.delta_hi[:, :], w.delta_lo[:, :])
        x, z, one_z, num = (self.temp.take() for _ in range(4))
        delta, du = self.delta.take(), self.du.take()
        v = lambda s: s.view[:, :]
        t = act.do(lambda e: e.activation(v(x), bank.view, ACT.Identity, bias=w.b_delta[:, 0:1]), done, *x.free)
        bank.free = [t]
        x_in = t
        t = dve.do(lambda e: e.scalar_tensor_tensor(v(z), v(x), -1.0, v(x), ALU.mult, ALU.min), t, *z.free)
        z_in = act.do(lambda e: e.activation(v(z), v(z), ACT.Exp), t)
        yield
        t = pool.do(lambda e: e.tensor_scalar(v(one_z), v(z), 1.0, 1.0, ALU.mult, ALU.add), z_in, *one_z.free)
        log = act.do(lambda e: e.activation(v(num), v(one_z), ACT.Ln), t, *num.free)
        t = pool.do(lambda e: e.tensor_scalar(v(one_z), v(one_z), 1.0, -1.0, ALU.mult, ALU.add), log)
        m = dve.do(lambda e: e.tensor_scalar(v(delta), v(one_z), 0.0, None, ALU.is_equal), t, *delta.free)
        yield
        t = pool.do(lambda e: e.tensor_tensor(v(one_z), v(one_z), v(delta), ALU.add), m)
        t2 = pool.do(lambda e: e.tensor_tensor(v(num), v(num), v(delta), ALU.add), m, log)
        t2 = pool.do(lambda e: e.tensor_tensor(v(num), v(num), v(z), ALU.mult), t2)
        t = dve.do(lambda e: e.reciprocal(v(one_z), v(one_z)), t)
        t = pool.do(lambda e: e.tensor_tensor(v(num), v(num), v(one_z), ALU.mult), t, t2)
        z.free, one_z.free = [t], [t]
        delta_in = dve.do(lambda e: e.scalar_tensor_tensor(v(delta), v(x), 0.0, v(num), ALU.max, ALU.add), t, x_in)
        x.free, num.free = [delta_in], [delta_in]
        yield
        du_in = pool.do(lambda e: e.tensor_tensor(v(du), v(delta), v(u), ALU.mult), delta_in, u_ready, *du.free)
        st["delta"], st["delta_ready"], st["du"], st["du_ready"] = delta, delta_in, du, du_in
        for m, (name, r) in enumerate((("bb", self.bb), ("cc", self.cc))):
            yield
            s = r.take()
            done = from_u(w.bc_hi[:, m, :], w.bc_lo[:, m, :])
            t = act.do(lambda e, s=s: e.activation(s.view[:, :], bank.view, ACT.Copy), done, *s.free)
            t = dve.do(lambda e, s=s: e.tensor_tensor(s.view[STATES:P, :], bank.view[STATES:P, :], f32(s.view[STATES:P, :]), ALU.subtract), t)
            bank.free = [t]
            st[name], st[name + "_ready"] = s, t
        u_hi.free = [done]
        return st

    def finish_chunk(self, chunk, st):
        core, w = self.core, self.w
        pe, act, dve, pool, sp = core.lanes
        y, g_hi, g_lo = self.temp.take(), self.u_hi.take(), self.u_lo.take()
        u, gate, xs = st["u"], st["gate"], st["xn"]
        t = dve.do(lambda e: e.scalar_tensor_tensor(y.view[:, :], u.view[:, :], w.skip[:, 0:1], self.y_bank.view, ALU.mult, ALU.add),
                   st["y_done"], *y.free)
        self.y_bank.free, u.free = [t], [t]
        yield
        t = pool.do(lambda e: e.tensor_tensor(y.view[:, :], y.view[:, :], gate.view[:, :], ALU.mult), t, st["gate_ready"])
        gate.free = [t]
        split = split_weights_on_pool(core, y.view[:, :], g_hi.view[:, :], g_lo.view[:, :], t, *g_hi.free)
        y.free = [split]
        bank = self.bank
        for pair in range(GT // 2):
            yield
            for k in range(2):
                j = 2 * pair + k
                rows = slice(j * P, (j + 1) * P)
                out = bank.view[:, k * D:(k + 1) * D]
                for n, (gs, ws) in enumerate(((g_hi, w.down_hi), (g_hi, w.down_lo), (g_lo, w.down_hi))):
                    done = pe.do(lambda e, n=n, gs=gs, ws=ws, rows=rows, out=out: e.matmul(out, gs.view[:, rows], ws[:, :], start=(n == 0), stop=(n == 2)),
                                 split, *bank.free, signal=(n == 2 and k == 1))
            o = self.out.take()
            psum = bank.view.rearrange("p (t d) -> p t d", t=2)
            t = dve.do(lambda e, o=o, psum=psum, pair=pair: e.tensor_tensor(o.view[:, :, :], psum, xs.view[:, 2 * pair:2 * pair + 2, :], ALU.add),
                       done, *o.free)
            bank.free = [t]
            t2 = pool.do(lambda e, o=o: e.tensor_tensor(o.view[:, :, :], o.view[:, :, :], w.b_down[:, :].unsqueeze(1).broadcast_to([P, 2, D]), ALU.add), t)
            rows = self.s_dram[chunk * CHUNK + pair * 2 * P:chunk * CHUNK + (pair + 1) * 2 * P, :]
            o.free = [sp.dma(o.dma_sem, lambda e, rows=rows, o=o: e.dma_start(rows.rearrange("(j p) d -> p j d", p=P), o.view[:, :, :]), t2)]
        g_hi.free = [done]
        xs.free = [t]

    def thread(self):
        core, w = self.core, self.w
        pe, act, dve, pool, sp = core.lanes
        items = [(k, n) for k in range(BATCH * CHUNKS) for n in range(STATES)]
        chunks = {0: finish(self.prepare(0))}
        work = {}
        helpers = []

        def broadcast(i, what, ring):
            k, n = items[i]
            st = chunks[k]
            s = ring.take()
            work[i][what] = s
            src = st[what]
            work[i][what + "_done"] = pe.do(lambda e: e.matmul(s.view, w.select[:, n:n + 1].broadcast_to([P, P]), src.view[:, :], start=True, stop=True),
                                            st[what + "_ready"], *s.free)
            if n == STATES - 1:
                src.free = [work[i][what + "_done"]]

        def decay(i):
            k, n = items[i]
            st, it = chunks[k], work[i]
            s = self.decay.take()
            it["decay"] = s
            it["decay_done"] = act.do(lambda e: e.activation(s.view[:, :], st["delta"].view[:, :], ACT.Exp, scale=w.a[:, n:n + 1]),
                                      st["delta_ready"], *s.free)
            if n == STATES - 1:
                st["delta"].free = [it["decay_done"]]

        def drive(i):
            k, n = items[i]
            st, it = chunks[k], work[i]
            s = self.drive.take()
            it["drive"] = s
            t = dve.do(lambda e: e.tensor_tensor(s.view[:, :], it["bb"].view, st["du"].view[:, :], ALU.mult), it["bb_done"], st["du_ready"], *s.free)
            it["bb"].free, it["drive_done"] = [t], t
            if n == STATES - 1:
                st["du"].free = [t]

        def recur(i):
            k, n = items[i]
            it = work[i]
            s = self.h.take()
            it["h"] = s
            start = 0.0 if k % CHUNKS == 0 else self.state[:, n:n + 1]
            t = dve.do(lambda e: e.tensor_tensor_scan(s.view[:, :], it["decay"].view[:, :], it["drive"].view[:, :], start, ALU.mult, ALU.add),
                       it["decay_done"], it["drive_done"], self.state_free.get(n), *s.free)
            it["decay"].free, it["drive"].free, it["h_done"] = [t], [t], t
            self.state_free[n] = it["kept"] = pool.do(lambda e: e.tensor_scalar(self.state[:, n:n + 1], s.view[:, CHUNK - 1:CHUNK], 1.0, 0.0, ALU.mult, ALU.add), t)

        def read_out(i):
            it = work[i]
            s = self.ch.take()
            it["ch"] = s
            t = dve.do(lambda e: e.tensor_tensor(s.view[:, :], it["cc"].view, it["h"].view[:, :], ALU.mult), it["cc_done"], it["h_done"], *s.free)
            it["cc"].free, it["ch_done"] = [t], t
            it["h"].free = [t, it["kept"]]

        def add_up(i):
            k, n = items[i]
            it = work.pop(i)
            t = pe.do(lambda e: e.matmul(self.y_bank.view, self.consts.identity[:, :], it["ch"].view[:, :], start=(n == 0), stop=(n == STATES - 1)),
                      it["ch_done"], *(self.y_bank.free if n == 0 else []))
            it["ch"].free = [t]
            if n == STATES - 1:
                chunks[k]["y_done"] = t
                end = self.finish_chunk(k, chunks.pop(k))
                next(end)
                helpers.insert(0, end)

        prep = None
        total = len(items)
        for i in range(-1, total + 3):
            if 0 <= i + 1 < total:
                k, n = items[i + 1]
                if n == 0 and k > 0:
                    while helpers:
                        finish(helpers.pop(0))
                    chunks[k] = prep[1] if prep[1] is not None else finish(prep[0])
                if n == 8 and k + 1 < BATCH * CHUNKS:
                    prep = [self.prepare(k + 1), None]
                work[i + 1] = {}
                broadcast(i + 1, "bb", self.b_banks)
                decay(i + 1)
            if 0 <= i < total:
                drive(i)
            if 0 <= i - 1 < total:
                broadcast(i - 1, "cc", self.c_banks)
                recur(i - 1)
            if 0 <= i - 2 < total:
                read_out(i - 2)
            if 0 <= i - 3 < total:
                add_up(i - 3)
            if helpers:
                if next(helpers[0], "end") == "end":
                    helpers.pop(0)
            elif prep is not None and prep[1] is None and items[min(i + 1, total - 1)][1] > 8 and i % 3 == 0:
                try:
                    next(prep[0])
                except StopIteration as e:
                    prep[1] = e.value
            yield
        while helpers:
            finish(helpers.pop(0))


class Experts:

    def __init__(self, core, ctx, consts, banks, a, xn_dram, acc_dram, list_dram):
        self.core, self.consts, self.a = core, consts, a
        self.xn_dram, self.acc_dram, self.list_dram = xn_dram, acc_dram, list_dram
        self.banks = Ring([Slot(banks[6][:, :]), Slot(banks[7][:, :])])
        self.xs = core.dma_ring(ctx, "moe_x", 2, [P, GT, D], F32)
        self.xt_hi = core.ring(ctx, "moe_xt_hi", 1, [P, DC, CAPACITY], F32R)
        self.xt_lo = core.ring(ctx, "moe_xt_lo", 1, [P, DC, CAPACITY], F32R)
        self.g = core.ring(ctx, "moe_g", 2, [P, HB, CAPACITY], F32)
        self.u = core.ring(ctx, "moe_u", 1, [P, HB, CAPACITY], F32)
        self.h_hi = core.ring(ctx, "moe_h_hi", 1, [P, HB, CAPACITY], F32R)
        self.h_lo = core.ring(ctx, "moe_h_lo", 1, [P, HB, CAPACITY], F32R)
        self.out = core.dma_ring(ctx, "moe_out", 2, [P, 2, D], F32)
        self.scores = core.sb(ctx, "moe_scores", [P, LISTS, TILES], F32)
        self.rows = core.sb(ctx, "moe_rows", [P, LISTS * SLOT_TILES], U32)
        self.weight = core.sb(ctx, "moe_weight", [P, LISTS * SLOT_TILES], F32)

    def turn(self, xs, ready):
        core = self.core
        hi, lo = self.xt_hi.take(), self.xt_lo.take()
        for c in range(DC):
            bank = self.banks.take()
            for j in range(GT):
                done = core.pe.do(lambda e, j=j, c=c, bank=bank: e.transpose(
                    bank.view[:, j * P:(j + 1) * P], xs.view[:, j, c * P:(c + 1) * P], self.consts.identity[:, :]),
                    *ready, *bank.free, signal=(j == GT - 1))
            split = split_from_psum(core, bank.view, hi.view[:, c, :], lo.view[:, c, :], done, *hi.free)
            bank.free = [split]
            yield
        xs.free = [done]
        return hi, lo, split

    def up(self, xt, wg, wu):
        core = self.core
        hi, lo, ready = xt
        g, u, h_hi, h_lo = self.g.take(), self.u.take(), self.h_hi.take(), self.h_lo.take()
        for f in range(HB):
            for w, out in ((wg, g), (wu, u)):
                bank = self.banks.take()
                parts = [(c, ws, xs) for c in range(DC) for ws, xs in ((w["hi"], hi), (w["hi"], lo), (w["lo"], hi))]
                for n, (c, ws, xs) in enumerate(parts):
                    done = core.pe.do(lambda e, n=n, c=c, ws=ws, xs=xs, bank=bank, f=f: e.matmul(
                        bank.view, ws[:, c, f * P:(f + 1) * P], xs.view[:, c, :], start=(n == 0), stop=(n == len(parts) - 1)),
                        ready, w["ready"], *bank.free, signal=(n == len(parts) - 1))
                t = core.act.do(lambda e, bank=bank, out=out, f=f: e.activation(out.view[:, f, :], bank.view, ACT.Copy), done, *out.free)
                bank.free = [t]
                yield
        hi.free = [done]
        t = core.act.do(lambda e: e.activation(g.view[:, :, :], g.view[:, :, :], ACT.Gelu), t)
        t = core.pool.do(lambda e: e.tensor_tensor(g.view[:, :, :], g.view[:, :, :], u.view[:, :, :], ALU.mult), t)
        u.free = [t]
        split = split_weights_on_pool(core, g.view[:, :, :], h_hi.view[:, :, :], h_lo.view[:, :, :], t, *h_hi.free)
        g.free = [split]
        return h_hi, h_lo, split, done

    def down(self, h, wd, emit):
        core = self.core
        hi, lo, ready, _ = h
        for pair in range(GT // 2):
            bank = self.banks.take()
            for k in range(2):
                j = 2 * pair + k
                rows = slice(j * P, (j + 1) * P)
                out = bank.view[:, k * D:(k + 1) * D]
                parts = [(f, hs, ws) for f in range(HB) for hs, ws in ((hi, wd["hi"]), (hi, wd["lo"]), (lo, wd["hi"]))]
                for n, (f, hs, ws) in enumerate(parts):
                    done = core.pe.do(lambda e, n=n, f=f, hs=hs, ws=ws, rows=rows, out=out: e.matmul(
                        out, hs.view[:, f, rows], ws[:, f, :], start=(n == 0), stop=(n == len(parts) - 1)),
                        ready, wd["ready"], *bank.free, signal=(n == len(parts) - 1))
                    if n == len(parts) // 2:
                        yield
                yield
            bank.free = [emit(pair, bank.view.rearrange("p (t d) -> p t d", t=2), done)]
        hi.free = [done]
        return done

    def shared(self):
        core, consts, a = self.core, self.consts, self.a
        pe, act, dve, pool, sp = core.lanes
        with ExitStack() as ctx:
            gate_raw = core.sb(ctx, "gate_raw", [P, DC, EXPERTS], F32)
            gate_hi = core.sb(ctx, "gate_hi", [P, DC, EXPERTS], F32R)
            gate_lo = core.sb(ctx, "gate_lo", [P, DC, EXPERTS], F32R)
            logits = core.ring(ctx, "logits", 2, [P, GT, EXPERTS], F32)
            small = core.ring(ctx, "softmax_small", 2, [P, 2, GT], F32)
            raw = core.dma_ring(ctx, "shared_raw", 1, [P, 1024], F32)
            w = {}
            for name, blocks, cols in (("Ws_gT", DC, HIDDEN), ("Ws_uT", DC, HIDDEN), ("Ws_dT", HB, D)):
                hi = core.sb(ctx, f"{name}_hi", [P, blocks, cols], F32R)
                lo = core.sb(ctx, f"{name}_lo", [P, blocks, cols], F32R)
                s = raw.take()
                v = s.view[:, :].rearrange("p (c n) -> p c n", c=blocks)
                t = sp.dma(s.dma_sem, lambda e, v=v, name=name: e.dma_start(v, a[name].rearrange("(c p) n -> p c n", p=P)), *s.free)
                t = split_weights_on_pool(core, v, hi[:, :, :], lo[:, :, :], t)
                s.free = [t]
                w[name] = {"hi": hi, "lo": lo, "ready": t}
                yield
            gate_dma = DmaSem(core, "gate_dma")
            t = sp.dma(gate_dma, lambda e: e.dma_start(gate_raw[:, :, :], a["gateT"].rearrange("(c p) n -> p c n", p=P)))
            gate_ready = split_weights_on_pool(core, gate_raw[:, :, :], gate_hi[:, :, :], gate_lo[:, :, :], t)

            def load(group):
                xs = self.xs.take()
                rows = self.xn_dram[group * GROUP:(group + 1) * GROUP, :]
                return xs, sp.dma(xs.dma_sem, lambda e: e.dma_start(xs.view[:, :, :], rows.rearrange("(j p) d -> p j d", p=P)), *xs.free)

            def gate(group, xt):
                hi, lo, ready = xt
                bank = self.banks.take()
                for j in range(GT):
                    rows = slice(j * P, (j + 1) * P)
                    parts = [(c, xs, ws) for c in range(DC) for xs, ws in ((hi, gate_hi), (hi, gate_lo), (lo, gate_hi))]
                    for n, (c, xs, ws) in enumerate(parts):
                        done = pe.do(lambda e, n=n, j=j, c=c, xs=xs, ws=ws, rows=rows: e.matmul(
                            bank.view[:, j * EXPERTS:(j + 1) * EXPERTS], xs.view[:, c, rows], ws[:, c, :], start=(n == 0), stop=(n == len(parts) - 1)),
                            ready, gate_ready, *bank.free, signal=(j == GT - 1 and n == len(parts) - 1))
                lg, sm = logits.take(), small.take()
                psum = bank.view[:, 0:GT * EXPERTS].rearrange("p (j e) -> p j e", j=GT)
                yield
                t = act.do(lambda e: e.activation(lg.view[:, :, :], psum, ACT.Copy), done, *lg.free)
                bank.free = [t]
                wide = lambda row: sm.view[:, row, :].unsqueeze(2).broadcast_to([P, GT, EXPERTS])
                t = dve.do(lambda e: e.tensor_reduce(sm.view[:, 0, :], lg.view[:, :, :], AX_X, ALU.max), t)
                t = dve.do(lambda e: e.tensor_tensor(lg.view[:, :, :], lg.view[:, :, :], wide(0), ALU.subtract), t)
                t = act.do(lambda e: e.activation(lg.view[:, :, :], lg.view[:, :, :], ACT.Exp), t)
                yield
                t = dve.do(lambda e: e.tensor_reduce(sm.view[:, 1, :], lg.view[:, :, :], AX_X, ALU.add), t)
                t = dve.do(lambda e: e.reciprocal(sm.view[:, 1, :], sm.view[:, 1, :]), t)
                b, tile = divmod(group * GT, TILES)
                dst = self.scores[:, b * EXPERTS:(b + 1) * EXPERTS, tile:tile + GT].rearrange("p e j -> p j e")
                t = dve.do(lambda e: e.tensor_tensor(dst, lg.view[:, :, :], wide(1), ALU.mult), t)
                lg.free, self.scored = [t], t

            def keep(group):
                def emit(pair, psum, done):
                    o = self.out.take()
                    t = act.do(lambda e: e.activation(o.view[:, :, :], psum, ACT.Copy), done, *o.free)
                    rows = self.acc_dram[group * GROUP + pair * 2 * P:group * GROUP + (pair + 1) * 2 * P, :]
                    saved = sp.dma(o.dma_sem, lambda e: e.dma_start(rows.rearrange("(j p) d -> p j d", p=P), o.view[:, :, :]), t)
                    o.free = [saved]
                    self.shared_saved[o.dma_sem.sem.name] = saved
                    return t
                return emit

            self.shared_saved = {}
            xs, loaded = load(0)
            before = None
            for group in range(TOKENS // GROUP):
                ahead = load(group + 1) if group + 1 < TOKENS // GROUP else None
                xt = yield from self.turn(xs, [loaded])
                yield from gate(group, xt)
                h = yield from self.up(xt, w["Ws_gT"], w["Ws_uT"])
                yield from self.down(h, w["Ws_dT"], keep(group))
                if ahead is not None:
                    xs, loaded = ahead
            self.shared_done = core.pe.last

    def choose(self):
        core, consts = self.core, self.consts
        pe, act, dve, pool, sp = core.lanes
        with ExitStack() as ctx:
            sb = lambda name, shape, dt=F32: core.sb(ctx, name, shape, dt)
            wide = lambda t: t[:, :].unsqueeze(2).broadcast_to([P, LISTS, TILES])
            flat = lambda t: t[:, :, :].rearrange("p l t -> p (l t)")
            full = [P, LISTS, TILES]
            below = sb("below", [P, P])
            reset = sb("reset", full)
            bits, trial, step = sb("bits", [P, LISTS], I32), sb("trial", [P, LISTS], I32), sb("step", [P, LISTS], I32)
            count = sb("count", [P, LISTS])
            need = sb("need", [P, LISTS])
            above, equal, rank, tmp = sb("above", full), sb("equal", full), sb("rank", full), sb("tmp", full)
            row_i, iota_i = sb("row_i", [P, BATCH * TILES], I32), sb("iota_i", [P, COLS32], I32)
            row_f, iota_f = sb("row_f", [P, BATCH * TILES]), sb("iota_f", [P, COLS32])
            left = core.ring(ctx, "onehot_left", 2, [P, TILES, 2 * ROWS16], F32)
            right = core.ring(ctx, "onehot_right", 2, [P, TILES, COLS32], F32)
            lists = sb("lists", [2 * ROWS16, LISTS, COLS32])
            first = self.shared_done
            t = pool.do(lambda e: e.affine_select(out=below[:, :], in_=consts.ones[:, :], compare_op=ALU.is_gt, fill=0.0,
                                                  base=0, pattern=[[1, P]], channel_multiplier=-1), first)
            t2 = pool.do(lambda e: e.memset(reset[:, :, :], 1.0), first)
            t2 = pool.do(lambda e: e.memset(reset[:, :, 0:1], 0.0), t2)
            pool.do(lambda e: e.iota(row_i[:, :], [[P, BATCH * TILES]], base=0, channel_multiplier=1), first)
            t3 = pool.do(lambda e: e.iota(iota_i[:, :], [[1, COLS32]], base=0, channel_multiplier=0))
            t3 = dve.do(lambda e: e.tensor_copy(row_f[:, :], row_i[:, :]), t3, first)
            made = dve.do(lambda e: e.tensor_copy(iota_f[:, :], iota_i[:, :]), t2)
            b = dve.do(lambda e: e.memset(bits[:, :], 0))

            def total(mask_sum, ready):
                bank = self.banks.take()
                done = pe.do(lambda e: e.matmul(bank.view[:, 0:LISTS], consts.ones[:, :], mask_sum[:, :], start=True, stop=True), ready, *bank.free)
                return bank, done

            for bit in reversed(range(SCORE_BITS)):
                t = dve.do(lambda e, bit=bit: e.tensor_scalar(trial[:, :], bits[:, :], 1 << bit, None, ALU.bitwise_or), b)
                t = dve.do(lambda e: e.tensor_tensor(tmp[:, :, :], self.scores[:, :, :], wide(trial[:, :].bitcast(F32)), ALU.is_ge), t, self.scored)
                yield
                t = dve.do(lambda e: e.tensor_reduce(count[:, :], tmp[:, :, :], AX_X, ALU.add), t)
                bank, done = total(count, t)
                yield
                t = dve.do(lambda e, bank=bank, bit=bit: e.tensor_scalar(step[:, :], bank.view[:, 0:LISTS], float(CAPACITY), float(1 << bit), ALU.is_ge, ALU.mult), done)
                bank.free = [t]
                b = dve.do(lambda e: e.tensor_tensor(bits[:, :], bits[:, :], step[:, :], ALU.bitwise_or), t)
                yield
            threshold = bits[:, :].bitcast(F32)
            t = dve.do(lambda e: e.tensor_tensor(above[:, :, :], self.scores[:, :, :], wide(threshold), ALU.is_gt), b)
            e_in = dve.do(lambda e: e.tensor_tensor(equal[:, :, :], self.scores[:, :, :], wide(threshold), ALU.is_equal), b)
            yield
            t = dve.do(lambda e: e.tensor_reduce(count[:, :], above[:, :, :], AX_X, ALU.add), t)
            bank, done = total(count, t)
            t = dve.do(lambda e: e.tensor_scalar(need[:, :], bank.view[:, 0:LISTS], -1.0, float(CAPACITY), ALU.mult, ALU.add), done)
            bank.free = [t]
            needed = t

            def ranks(mask, ready):
                for half in range(2):
                    cols = slice(half * BANK, (half + 1) * BANK)
                    before, totals = self.banks.take(), self.banks.take()
                    d1 = pe.do(lambda e, cols=cols, before=before: e.matmul(before.view, below[:, :], flat(mask)[:, cols], start=True, stop=True), ready, made, *before.free)
                    d2 = pe.do(lambda e, cols=cols, totals=totals: e.matmul(totals.view, consts.ones[:, :], flat(mask)[:, cols], start=True, stop=True), *totals.free)
                    yield
                    t = dve.do(lambda e, cols=cols, totals=totals: e.tensor_tensor_scan(flat(rank)[:, cols], flat(reset)[:, cols], totals.view, 0.0, ALU.mult, ALU.add), d2)
                    t = dve.do(lambda e, cols=cols, totals=totals: e.tensor_tensor(flat(rank)[:, cols], flat(rank)[:, cols], totals.view, ALU.subtract), t)
                    totals.free = [t]
                    t = dve.do(lambda e, cols=cols, before=before: e.tensor_tensor(flat(rank)[:, cols], flat(rank)[:, cols], before.view, ALU.add), t)
                    before.free = [t]
                    yield
                return t

            t = yield from ranks(equal, e_in)
            t = dve.do(lambda e: e.tensor_tensor(tmp[:, :, :], rank[:, :, :], wide(need), ALU.is_lt), t, needed)
            t = dve.do(lambda e: e.tensor_tensor(tmp[:, :, :], tmp[:, :, :], equal[:, :, :], ALU.mult), t)
            t = dve.do(lambda e: e.tensor_tensor(above[:, :, :], above[:, :, :], tmp[:, :, :], ALU.add), t)
            yield
            r = yield from ranks(above, t)
            t = dve.do(lambda e: e.tensor_scalar(tmp[:, :, :], above[:, :, :], -2.0 * SEQ, 2.0 * SEQ, ALU.mult, ALU.add), t)
            t = dve.do(lambda e: e.tensor_tensor(rank[:, :, :], rank[:, :, :], tmp[:, :, :], ALU.add), t, r)
            yield
            as_int = tmp[:, :, :].bitcast(I32)
            t = dve.do(lambda e: e.tensor_copy(as_int, rank[:, :, :]), t)
            t = dve.do(lambda e: e.tensor_scalar(above[:, :, :].bitcast(I32), as_int, 5, None, ALU.logical_shift_right), t)
            t = dve.do(lambda e: e.tensor_copy(equal[:, :, :], above[:, :, :].bitcast(I32)), t)
            yield
            t = dve.do(lambda e: e.tensor_scalar(above[:, :, :].bitcast(I32), as_int, COLS32 - 1, None, ALU.bitwise_and), t)
            ready = dve.do(lambda e: e.tensor_copy(rank[:, :, :], above[:, :, :].bitcast(I32)), t)
            list_row, list_col = equal, rank
            copied = []
            for l in range(LISTS):
                yield
                A, C = left.take(), right.take()
                hot = A.view[:, :, ROWS16:2 * ROWS16]
                over_tiles = lambda ap, n: ap.unsqueeze(2).broadcast_to([P, TILES, n])
                over_cols = lambda ap, n: ap.unsqueeze(1).broadcast_to([P, TILES, n])
                t = dve.do(lambda e, l=l, hot=hot: e.tensor_tensor(hot, over_tiles(list_row[:, l, :], ROWS16), over_cols(iota_f[:, 0:ROWS16], ROWS16), ALU.is_equal),
                            ready, made, *A.free)
                tiles = slice((l // EXPERTS) * TILES, (l // EXPERTS + 1) * TILES)
                t = pool.do(lambda e, hot=hot, A=A, tiles=tiles: e.tensor_tensor(A.view[:, :, 0:ROWS16], hot, over_tiles(row_f[:, tiles], ROWS16), ALU.mult), t, t3)
                t = pool.do(lambda e, l=l, hot=hot: e.tensor_tensor(hot, hot, over_tiles(self.scores[:, l, :], ROWS16), ALU.mult), t)
                yield
                t2 = dve.do(lambda e, l=l, C=C: e.tensor_tensor(C.view[:, :, :], over_tiles(list_col[:, l, :], COLS32), over_cols(iota_f[:, :], COLS32), ALU.is_equal),
                             ready, made, *C.free)
                bank = self.banks.take()
                for k in range(TILES):
                    done = pe.do(lambda e, k=k, A=A, C=C, bank=bank: e.matmul(bank.view[0:2 * ROWS16, 0:COLS32], A.view[:, k, :], C.view[:, k, :],
                                                                             start=(k == 0), stop=(k == TILES - 1)), t, t2, *bank.free, signal=(k == TILES - 1))
                    if k % 8 == 7:
                        yield
                A.free, C.free = [done], [done]
                t = act.do(lambda e, l=l, bank=bank: e.activation(lists[:, l, :], bank.view[0:2 * ROWS16, 0:COLS32], ACT.Copy), done)
                bank.free = [t]
            lists_dma = DmaSem(core, "lists_dma")
            for kind in range(2):
                out = self.list_dram[kind].rearrange("l (a c) -> a l c", a=ROWS16)
                t2 = sp.dma(lists_dma, lambda e, kind=kind, out=out: e.dma_start(out, lists[kind * ROWS16:(kind + 1) * ROWS16, :, :]), t)
            back_dma = DmaSem(core, "lists_back_dma")
            slots = lambda kind: self.list_dram[kind].rearrange("l (p j) -> p l j", p=P)
            as_lists = lambda ap: ap.rearrange("p (l j) -> p l j", j=SLOT_TILES)
            rows_f = tmp[:, 0:SLOT_TILES, :].rearrange("p a b -> p (a b)")
            sp.dma(back_dma, lambda e: e.dma_start(as_lists(rows_f), slots(0)), t2)
            t = sp.dma(back_dma, lambda e: e.dma_start(as_lists(self.weight[:, :]), slots(1)))
            self.chosen = dve.do(lambda e: e.tensor_copy(self.rows[:, :], rows_f), t)
            self.choose_done = [self.chosen, done, core.pool.last, core.act.last]
            yield

    def experts(self):
        core, a = self.core, self.a
        pe, act, dve, pool, sp = core.lanes
        with ExitStack() as ctx:
            raw = core.dma_ring(ctx, "expert_raw", 2, [P, 1024], F32)
            w_hi = core.ring(ctx, "expert_hi", 4, [P, 1024], F32R)
            w_lo = core.ring(ctx, "expert_lo", 4, [P, 1024], F32R)
            for s in raw.slots + w_hi.slots + w_lo.slots:
                s.free = list(self.choose_done)
            for s in self.xs.slots + self.out.slots:
                s.dma_sem = DmaSem(core, s.dma_sem.sem.name + "_indirect")
            indirect = lambda col: bass.IndirectOffsetOnAxis(ap=self.rows[:, col:col + 1], axis=0)

            def weights(name, expert, blocks):
                s, hi, lo = raw.take(), w_hi.take(), w_lo.take()
                v, h, l = (x.view[:, :].rearrange("p (c n) -> p c n", c=blocks) for x in (s, hi, lo))
                t = sp.dma(s.dma_sem, lambda e: e.dma_start(v, a[name][expert].rearrange("(c p) n -> p c n", p=P)), *s.free)
                t = split_weights_on_pool(core, v, h, l, t, *hi.free)
                s.free = [t]
                return {"hi": h, "lo": l, "ready": t, "slot": hi}

            def gather(l):
                xs = self.xs.take()
                for j in range(SLOT_TILES):
                    t = pool.dma(xs.dma_sem, lambda e, j=j: e.indirect_dma_start(
                        xs.view[:, j, :], None, self.xn_dram, indirect(l * SLOT_TILES + j)), self.chosen, *xs.free)
                return xs, t

            added = {}

            def scatter(l, expert):
                b = l // EXPERTS

                def emit(pair, psum, done):
                    o = self.out.take()
                    for k in range(2):
                        col = l * SLOT_TILES + 2 * pair + k
                        t = act.do(lambda e, k=k, col=col: e.activation(o.view[:, k, :], psum[:, k, :], ACT.Copy, scale=self.weight[:, col:col + 1]), done, *o.free)
                    before = [x for key, x in added.items() if key[0] == b and key[1] < expert]
                    for k in range(2):
                        col = l * SLOT_TILES + 2 * pair + k
                        s = pool.dma(o.dma_sem, lambda e, k=k, col=col: e.indirect_dma_start(
                            self.acc_dram, indirect(col), o.view[:, k, :], None, compute_op=ALU.add),
                            t, *before, *self.shared_saved.values())
                    o.free = [s]
                    added[b, expert, pair] = s
                    for key in [key for key in added if key[0] == b and key[1] < expert - 1]:
                        added.pop(key)
                    return t
                return emit

            order = [(expert, b) for expert in range(EXPERTS) for b in range(BATCH)]
            w = {0: {"g": weights("WgT", 0, DC), "u": weights("WuT", 0, DC), "d": weights("WdT", 0, HB)}}
            xs, loaded = gather(0)
            last = None
            for n, (expert, b) in enumerate(order):
                ahead = None
                if n + 1 < len(order):
                    e2, b2 = order[n + 1]
                    ahead = gather(b2 * EXPERTS + e2)
                xt = yield from self.turn(xs, [loaded])
                if b == BATCH - 1 and expert + 1 < EXPERTS:
                    w[expert + 1] = {"g": weights("WgT", expert + 1, DC)}
                h = yield from self.up(xt, w[expert]["g"], w[expert]["u"])
                if b == BATCH - 1:
                    w[expert]["g"]["slot"].free = [h[3]]
                    w[expert]["u"]["slot"].free = [h[3]]
                    if expert + 1 < EXPERTS:
                        w[expert + 1]["u"] = weights("WuT", expert + 1, DC)
                        w[expert + 1]["d"] = weights("WdT", expert + 1, HB)
                done = yield from self.down(h, w[expert]["d"], scatter(b * EXPERTS + expert, expert))
                if b == BATCH - 1:
                    w[expert]["d"]["slot"].free = [done]
                    w.pop(expert)
                if ahead is not None:
                    xs, loaded = ahead

    def thread(self):
        yield from self.shared()
        yield from self.choose()
        yield from self.experts()


def layer1(core, consts, a, x1_dram, xn_dram, s_dram, acc_dram, list_dram, out_dram):
    with ExitStack() as stage:
        w = ScanWeights(core, stage, consts, a)
        banks = core.psum_banks(stage, "layer1")
        scan = SelectiveScan(core, stage, consts, w, banks, a, xn_dram, s_dram)
        moe = Experts(core, stage, consts, banks, a, xn_dram, acc_dram, list_dram)
        scan_steps, moe_steps = scan.thread(), moe.thread()
        for _ in scan_steps:
            next(moe_steps, None)
        finish(moe_steps)
        core.hand_over()
    combine(core, x1_dram, s_dram, acc_dram, out_dram)


def combine(core, x1_dram, s_dram, acc_dram, out_dram):
    pe, act, dve, pool, sp = core.lanes
    with ExitStack() as ctx:
        x_ring = core.dma_ring(ctx, "final_x", 3, [P, GT, D], F32)
        s_ring = core.dma_ring(ctx, "final_s", 3, [P, GT, D], F32)
        m_ring = core.dma_ring(ctx, "final_m", 3, [P, GT, D], F32)
        e_ring = core.ring(ctx, "final_e", 3, [P, GT, D], F32)
        for g in range(TOKENS // GROUP):
            rows = lambda dram: dram[g * GROUP:(g + 1) * GROUP, :].rearrange("(p j) d -> p j d", p=P)
            x, s, m, e = x_ring.take(), s_ring.take(), m_ring.take(), e_ring.take()
            v = lambda slot: slot.view[:, :, :]
            load = lambda slot, dram: sp.dma(slot.dma_sem, lambda q, slot=slot, src=rows(dram): q.dma_start(v(slot), src), *slot.free)
            tm, tx, ts = load(m, acc_dram), load(x, x1_dram), load(s, s_dram)
            t = act.do(lambda q, e=e, m=m: q.activation(v(e), v(m), ACT.Exp, scale=-1.0), tm, *e.free)
            t = dve.do(lambda q, e=e: q.tensor_scalar(v(e), v(e), 1.0, None, ALU.add), t)
            t = dve.do(lambda q, e=e: q.reciprocal(v(e), v(e)), t)
            t2 = pool.do(lambda q, s=s, m=m: q.tensor_tensor(v(s), v(s), v(m), ALU.mult), ts, tm)
            m.free = [t, t2]
            t = dve.do(lambda q, e=e, s=s: q.tensor_tensor(v(e), v(e), v(s), ALU.mult), t, t2)
            s.free = [t]
            t = dve.do(lambda q, e=e, x=x: q.tensor_tensor(v(x), v(x), v(e), ALU.add), t, tx)
            e.free = [t]
            x.free = [sp.dma(x.dma_sem, lambda q, x=x, dst=rows(out_dram): q.dma_start(dst, v(x)), t)]
        core.hand_over()


LAYER0_INPUTS = ("x", "qkv", "woT", "out_b", "w1", "w1T", "b1", "w2", "w2T", "b2")
LAYER1_INPUTS = ("ln_gamma", "ln_beta", "W_up", "b_up", "conv_w", "conv_b", "W_delta", "b_delta", "W_B", "W_C", "A_log", "D",
                 "W_down", "b_down", "gateT", "WgT", "WuT", "WdT", "Ws_gT", "Ws_uT", "Ws_dT")


def two_layers(nc, a, out_dram):
    scratch = lambda name, shape: nc.dram_tensor(name, shape, F32, kind="Internal").ap()
    q_dram = scratch("q_scratch", [BATCH * GROUPS, P, DC, GROUP])
    g_dram = scratch("g_scratch", [TOKENS, D])
    x1_dram = scratch("x1_scratch", [TOKENS, D])
    xn1_dram = scratch("xn1_scratch", [TOKENS, D])
    s_dram = scratch("s_scratch", [TOKENS, D])
    moe_dram = scratch("moe_scratch", [TOKENS, D])
    list_dram = scratch("list_scratch", [2, LISTS, CAPACITY])
    with ExitStack() as ctx:
        core = Core(nc, ctx)
        consts = Constants(core, ctx)
        with ExitStack() as layer0:
            w = Layer0Weights(core, layer0, consts, a)
            kv = KeysValues(core, layer0)
            for b in range(BATCH):
                binary_ffn_and_qkv(core, consts, w, kv, b, a["x"], q_dram, g_dram)
                attention(core, consts, w, kv, b, a["x"], q_dram, g_dram, x1_dram, xn1_dram)
        layer1(core, consts, a, x1_dram, xn1_dram, s_dram, moe_dram, list_dram, out_dram)
        core.sp.do(lambda e: e.drain())
        core.run()


def kernel(**inputs):
    import numpy as np
    import concourse.bacc as bacc
    from concourse.bass_utils import run_bass_kernel_spmd

    rest = slice(D // 4, 3 * D // 4)
    order = np.concatenate([np.arange(0, D // 4), np.arange(3 * D // 4, D), np.arange(rest.start, rest.stop)])
    l0a, l0f = (lambda n: np.asarray(inputs["L0_attn_" + n])), (lambda n: np.asarray(inputs["L0_ffn_" + n]))
    l1a, l1f = (lambda n: np.asarray(inputs["L1_attn_" + n])), (lambda n: np.asarray(inputs["L1_ffn_" + n]))
    arrays = {
        "x": l0a("x").reshape(TOKENS, D)[:, order],
        "qkv": l0a("weight_qkv")[order],
        "woT": l0a("out_w").T[:, order],
        "out_b": l0a("out_b")[order],
        "w1": l0f("w1")[:, order],
        "w1T": l0f("w1").T[order],
        "b1": l0f("b1"),
        "w2": l0f("w2")[order],
        "w2T": l0f("w2").T[:, order],
        "b2": l0f("b2")[order],
        "ln_gamma": l1a("ln_gamma")[order],
        "ln_beta": l1a("ln_beta")[order],
        "W_up": l1a("W_up")[order],
        "b_up": l1a("b_up"),
        "conv_w": l1a("conv_w")[:, 0, :],
        "conv_b": l1a("conv_b"),
        "W_delta": l1a("W_delta"),
        "b_delta": l1a("b_delta"),
        "W_B": l1a("W_B"),
        "W_C": l1a("W_C"),
        "A_log": l1a("A_log"),
        "D": l1a("D"),
        "W_down": l1a("W_down")[:, order],
        "b_down": l1a("b_down")[order],
        "gateT": l1f("gate_w")[:, order].T,
        "WgT": l1f("Wg")[:, :, order].transpose(0, 2, 1),
        "WuT": l1f("Wu")[:, :, order].transpose(0, 2, 1),
        "WdT": l1f("Wd")[:, order, :].transpose(0, 2, 1),
        "Ws_gT": l1f("Ws_g")[:, order].T,
        "Ws_uT": l1f("Ws_u")[:, order].T,
        "Ws_dT": l1f("Ws_d")[order].T,
    }
    nc = bacc.Bacc("TRN2", target_bir_lowering=False, num_devices=1)
    a = {}
    for name in LAYER0_INPUTS + LAYER1_INPUTS:
        arrays[name] = np.ascontiguousarray(arrays[name])
        a[name] = nc.dram_tensor(name, arrays[name].shape, mybir.dt.from_np(arrays[name].dtype), kind="ExternalInput").ap()
    out_dram = nc.dram_tensor("x2", [TOKENS, D], F32, kind="ExternalOutput").ap()
    two_layers(nc, a, out_dram)
    result = run_bass_kernel_spmd(nc, [arrays], core_ids=[0]).results[0]["x2"]
    out = np.empty_like(result)
    out[:, order] = result
    return out.reshape(BATCH, SEQ, D)
```

```python
from contextlib import ExitStack

import concourse.bass as bass
from concourse import mybir

F32 = mybir.dt.float32
F32R = mybir.dt.float32r
F16 = mybir.dt.float16
I32 = mybir.dt.int32
U32 = mybir.dt.uint32
ALU = mybir.AluOpType
ACT = mybir.ActivationFunctionType
AX_X = mybir.AxisListType.X

P = 128
BATCH = 2
SEQ = 4096
TOKENS = BATCH * SEQ
D = 256
DC = D // P
GROUP = 512
GT = GROUP // P
GROUPS = SEQ // GROUP
BANK = 512
LN_EPS = 1e-5
FFN_LAG = 2


class Lane:

    def __init__(self, nc, ctx, name):
        self.nc, self.ctx, self.name = nc, ctx, name
        self.queue = []
        self.waited = {}
        self.stage = 0
        self.fence = []
        self.last = None
        self.new_stage()

    def new_stage(self):
        self.sem = self.ctx.enter_context(self.nc.semaphore(f"{self.name}_done_{self.stage}"))
        self.count = 0
        self.stage += 1

    def _waits(self, waits):
        need = []
        for token in list(self.fence) + list(waits):
            if token is None:
                continue
            sem, value = token
            if self.waited.get(sem.name, (None, 0))[1] < value:
                self.waited[sem.name] = (sem, value)
                need = [n for n in need if n[0].name != sem.name] + [(sem, value)]
        self.fence = []
        return need

    def do(self, issue, *waits, signal=True):
        need = self._waits(waits)
        token = None
        if signal:
            self.count += 1
            token = self.last = (self.sem, self.count)
        self.queue.append((need, issue, self.sem if signal else None, 1))
        return token

    def dma(self, slot_sem, issue, *waits):
        need = self._waits(waits)
        slot_sem.count += 16
        self.queue.append((need, issue, slot_sem.sem, 16))
        return (slot_sem.sem, slot_sem.count)

    def replay(self, engine):
        for need, issue, sem, by in self.queue:
            for wait_sem, value in need:
                engine.wait_ge(wait_sem, value)
            done = issue(engine) if issue is not None else None
            if sem is not None:
                done.then_inc(sem, by)


class DmaSem:
    def __init__(self, core, name):
        self.sem = core.ctx.enter_context(core.nc.semaphore(name))
        self.count = 0
        core.dma_sems.append(self)

    def token(self):
        return (self.sem, self.count)


class Slot:

    def __init__(self, view, dma_sem=None):
        self.view, self.free, self.dma_sem = view, [], dma_sem


class Ring:
    def __init__(self, slots):
        self.slots, self.at = slots, -1

    def take(self):
        self.at += 1
        return self.slots[self.at % len(self.slots)]


class Core:

    def __init__(self, nc, ctx):
        self.nc, self.ctx, self.dma_sems = nc, ctx, []
        self.pe = Lane(nc, ctx, "pe")
        self.act = Lane(nc, ctx, "act")
        self.dve = Lane(nc, ctx, "dve")
        self.pool = Lane(nc, ctx, "pool")
        self.sp = Lane(nc, ctx, "sp")
        self.lanes = [self.pe, self.act, self.dve, self.pool, self.sp]

    def psum_banks(self, ctx, stage):
        return [ctx.enter_context(self.nc.psum_tensor(f"{stage}_bank{i}", [P, BANK], F32)) for i in range(8)]

    def sb(self, ctx, name, shape, dtype):
        return ctx.enter_context(self.nc.sbuf_tensor(f"{name}_sb", shape, dtype))

    def dma_ring(self, ctx, name, n, shape, dtype):
        return Ring([Slot(self.sb(ctx, f"{name}{i}", shape, dtype), DmaSem(self, f"{name}_dma{i}")) for i in range(n)])

    def ring(self, ctx, name, n, shape, dtype):
        return Ring([Slot(self.sb(ctx, f"{name}{i}", shape, dtype)) for i in range(n)])

    def hand_over(self):
        every = [lane.last for lane in self.lanes if lane.last] + [d.token() for d in self.dma_sems if d.count]
        for lane in self.lanes:
            lane.fence = list(every)
            lane.new_stage()
            lane.last = None

    def run(self):
        block = self.ctx.enter_context(self.nc.Block())
        block.tensor(self.pe.replay)
        block.scalar(self.act.replay)
        block.vector(self.dve.replay)
        block.gpsimd(self.pool.replay)
        block.sync(self.sp.replay)


def f32(view):
    return view.bitcast(F32)


def split_weights(core, src, hi, lo, *waits):
    th = core.dve.do(lambda e: e.tensor_copy(hi, src), *waits)
    return core.dve.do(lambda e: e.tensor_tensor(lo, src, f32(hi), ALU.subtract), th)


def split_weights_on_pool(core, src, hi, lo, *waits):
    th = core.pool.do(lambda e: e.tensor_scalar(hi, src, 1.0, 0.0, ALU.mult, ALU.add), *waits)
    return core.pool.do(lambda e: e.tensor_tensor(lo, src, f32(hi), ALU.subtract), th)


def split_from_psum(core, bank, hi, lo, matmul_done, *free):
    th = core.act.do(lambda e: e.activation(hi, bank, ACT.Copy), matmul_done, *free)
    return core.dve.do(lambda e: e.tensor_tensor(lo, bank, f32(hi), ALU.subtract), th, *free)


class Constants:
    def __init__(self, core, ctx):
        nc, pool = core.nc, core.pool
        self.identity = core.sb(ctx, "identity", [P, P], F32)
        self.ones = core.sb(ctx, "ones", [P, P], F32)
        self.minus_half = core.sb(ctx, "minus_half", [P, GT], F32)
        t = pool.do(lambda e: e.memset(self.identity[:, :], 0.0))
        pool.do(lambda e: e.memset(self.ones[:, :], 1.0))
        pool.do(lambda e: e.memset(self.minus_half[:, :], -0.5))
        self.ready = pool.do(lambda e: e.affine_select(
            out=self.identity[:, :], in_=self.identity[:, :], compare_op=ALU.not_equal, fill=1.0,
            base=0, pattern=[[-1, P]], channel_multiplier=1), t)


class LayerNorm:

    def __init__(self, core, ctx, consts, name, n=2):
        self.core, self.consts = core, consts
        self.stats = core.ring(ctx, f"{name}_stats", n, [P, GT, 6], F32)
        self.moments = core.ring(ctx, f"{name}_moments", n, [P, GT, 2], F32)
        self.rstd = core.ring(ctx, f"{name}_rstd", n, [P, 2, GT], F32)

    def __call__(self, src, dst, src_ready, *dst_free):
        return self.apply(self.statistics(src, src_ready), src, dst, *dst_free)

    def statistics(self, src, src_ready):
        core, consts, tiles = self.core, self.consts, len(src)
        st, mo, rs = self.stats.take(), self.moments.take(), self.rstd.take()
        free = list(st.free)
        aggr = None
        for j in range(tiles):
            t = core.dve.do(lambda e, j=j: e.bn_stats(st.view[:, j, :], src[j]), src_ready, *free)
            aggr = core.dve.do(lambda e, j=j: e.bn_aggr(mo.view[:, j, :], st.view[:, j, :]), t)
        ve, r = rs.view[:, 0, 0:tiles], rs.view[:, 1, 0:tiles]
        t = core.pool.do(lambda e: e.tensor_scalar(ve, mo.view[:, 0:tiles, 1], LN_EPS, None, ALU.add), aggr, *free)
        t = core.pool.do(lambda e: e.tensor_tensor(r, ve, consts.minus_half[:, 0:tiles], ALU.pow), t, consts.ready)
        return st, mo, rs, t

    def apply(self, measured, src, dst, *dst_free):
        core = self.core
        st, mo, rs, t = measured
        for j in range(len(src)):
            last = core.dve.do(lambda e, j=j: e.tensor_scalar(
                dst[j], src[j], mo.view[:, j, 0:1], rs.view[:, 1, j:j + 1], ALU.subtract, ALU.mult), t, *dst_free)
        st.free = [last]
        return last


def binary_ffn_and_qkv(core, consts, w, kv, b, x_dram, q_dram, g_dram):
    with ExitStack() as ctx:
        banks = core.psum_banks(ctx, f"ffn{b}")
        tr_ring = Ring([Slot(banks[0][:, :]), Slot(banks[1][:, :])])
        mm_ring = Ring([Slot(banks[2][:, :]), Slot(banks[3][:, :])])
        hid_ring = Ring([Slot(banks[4][:, :]), Slot(banks[5][:, :])])
        out_banks = [Slot(banks[6][:, :]), Slot(banks[7][:, :])]
        x_ring = core.dma_ring(ctx, f"x_b{b}_", 2, [P, GT, D], F32)
        xt_hi = core.ring(ctx, f"xt_hi_b{b}_", 2, [P, DC, GROUP], F32R)
        xt_lo = core.ring(ctx, f"xt_lo_b{b}_", 2, [P, DC, GROUP], F32R)
        xt_16 = core.ring(ctx, f"xt_16_b{b}_", 2, [P, GROUP], F16)
        q_ring = core.dma_ring(ctx, f"q_out_b{b}_", 1, [P, DC, GROUP], F32)
        g_ring = core.dma_ring(ctx, f"g_out_b{b}_", 1, [P, GT, D], F32)
        h_ring = core.ring(ctx, f"h_b{b}_", 1, [P, GROUP], F32)
        h_hi = core.ring(ctx, f"h_hi_b{b}_", FFN_LAG + 1, [P, GROUP], F32R)
        h_lo = core.ring(ctx, f"h_lo_b{b}_", FFN_LAG + 1, [P, GROUP], F32R)
        norm = LayerNorm(core, ctx, consts, f"ln0_b{b}", 1)

        def load_group(g):
            xs = x_ring.take()
            rows = x_dram[(b * GROUPS + g) * GROUP:(b * GROUPS + g + 1) * GROUP, :]
            loaded = core.sp.dma(xs.dma_sem, lambda e: e.dma_start(
                xs.view[:, :, :], rows.rearrange("(j p) d -> p j d", p=P)), *xs.free)
            tiles = [xs.view[:, j, :] for j in range(GT)]
            for _ in range(4):
                yield
            measured = norm.statistics(tiles, loaded)
            yield
            normed = norm.apply(measured, tiles, tiles)
            yield
            yield
            hi, lo, half = xt_hi.take(), xt_lo.take(), xt_16.take()
            freed = []
            for c in range(DC):
                yield
                bank = tr_ring.take()
                for j in range(GT):
                    done = core.pe.do(lambda e, j=j, c=c, bank=bank: e.transpose(
                        bank.view[:, j * P:(j + 1) * P], xs.view[:, j, c * P:(c + 1) * P], consts.identity[:, :]),
                        normed, *bank.free, signal=(j == GT - 1))
                freed.append(done)
                if c == 0:
                    done = core.act.do(lambda e, bank=bank: e.activation(half.view[:, :], bank.view, ACT.Copy),
                                       done, *half.free)
                split = split_from_psum(core, bank.view, hi.view[:, c, :], lo.view[:, c, :], done, *hi.free)
                bank.free = [split]
            xs.free = freed
            return hi, lo, half, split

        def group(g, ready):
            hi, lo, half, split = ready

            def qk_block(col):
                bank = mm_ring.take()
                cols = slice(col, col + P)
                core.pe.do(lambda e: e.matmul(bank.view, w.qkv_16[:, cols], half.view[:, :], start=True, stop=False),
                           split, w.ready, *bank.free, signal=False)
                core.pe.do(lambda e: e.matmul(bank.view, w.qkv_hi[:, cols], hi.view[:, 1, :], start=False, stop=False), signal=False)
                core.pe.do(lambda e: e.matmul(bank.view, w.qkv_hi[:, cols], lo.view[:, 1, :], start=False, stop=False), signal=False)
                done = core.pe.do(lambda e: e.matmul(bank.view, w.qkv_lo[:, cols], hi.view[:, 1, :], start=False, stop=True))
                return bank, done

            q_out = q_ring.take()
            for m in range(DC):
                bank, done = qk_block(m * P)
                sent = core.act.do(lambda e, m=m, bank=bank: e.activation(
                    q_out.view[:, m, :], bank.view, ACT.Copy, scale=float(D) ** -0.5), done, *q_out.free)
                bank.free = [sent]
            q_out.free = [core.sp.dma(q_out.dma_sem, lambda e: e.dma_start(q_dram[b * GROUPS + g], q_out.view[:, :, :]), sent)]
            yield
            for m in range(DC):
                bank, done = qk_block(D + m * P)
                cols = slice(g * GROUP, (g + 1) * GROUP)
                bank.free = [split_from_psum(core, bank.view, kv.k_hi[:, m, cols], kv.k_lo[:, m, cols], done)]
            if emptied:
                scale_output()
            yield
            for pair in range(GT // 2):
                bank = mm_ring.take()
                for half_bank in range(2):
                    j = 2 * pair + half_bank
                    rows = slice(j * P, (j + 1) * P)
                    out = bank.view[:, half_bank * D:(half_bank + 1) * D]
                    core.pe.do(lambda e, rows=rows, out=out: e.matmul(out, half.view[:, rows], w.qkv_16[:, 2 * D:3 * D], start=True, stop=False),
                               *bank.free, signal=False)
                    core.pe.do(lambda e, rows=rows, out=out: e.matmul(out, hi.view[:, 1, rows], w.qkv_hi[:, 2 * D:3 * D], start=False, stop=False), signal=False)
                    core.pe.do(lambda e, rows=rows, out=out: e.matmul(out, hi.view[:, 1, rows], w.qkv_lo[:, 2 * D:3 * D], start=False, stop=False), signal=False)
                    done = core.pe.do(lambda e, rows=rows, out=out: e.matmul(out, lo.view[:, 1, rows], w.qkv_hi[:, 2 * D:3 * D], start=False, stop=True),
                                      signal=(half_bank == 1))
                blocks = slice(g * GT + 2 * pair, g * GT + 2 * pair + 2)
                psum = bank.view.rearrange("p (t d) -> p t d", t=2)
                bank.free = [split_weights(core, psum, kv.v[:, blocks, 0:D], kv.v[:, blocks, D:2 * D], done)]
            half.free = [done]
            waiting = []
            for f in range(w.hidden_blocks + FFN_LAG):
                yield
                if f == w.hidden_blocks and scaled:
                    gate_to_dram()
                if f < w.hidden_blocks:
                    bank = hid_ring.take()
                    for c in range(DC):
                        for part in (hi, lo):
                            last = c == DC - 1 and part is lo
                            done = core.pe.do(lambda e, f=f, c=c, part=part, bank=bank, last=last: e.matmul(
                                bank.view, w.sign1[:, c, f * P:(f + 1) * P], part.view[:, c, :],
                                start=(c == 0 and part is hi), stop=last), *bank.free, signal=last)
                    h, hh, hl = h_ring.take(), h_hi.take(), h_lo.take()
                    a = core.act.do(lambda e, f=f, bank=bank, hh=hh: e.activation(
                        hh.view[:, :], bank.view, ACT.Gelu, bias=w.b1[:, f:f + 1], scale=w.alpha1[:, f:f + 1]),
                        done, *hh.free)
                    a = core.act.do(lambda e, f=f, bank=bank, h=h: e.activation(
                        h.view[:, :], bank.view, ACT.Gelu, bias=w.b1[:, f:f + 1], scale=w.alpha1[:, f:f + 1]),
                        *h.free)
                    bank.free = [a]
                    l = core.dve.do(lambda e, h=h, hh=hh, hl=hl: e.tensor_tensor(
                        hl.view[:, :], h.view[:, :], f32(hh.view[:, :]), ALU.subtract), a, *hh.free)
                    h.free = [l]
                    waiting.append((hh, hl, l))
                    if f == w.hidden_blocks - 1:
                        hi.free = [done]
                if f >= FFN_LAG:
                    hh, hl, ready_h = waiting.pop(0)
                    block = f - FFN_LAG
                    for j in range(GT):
                        ob = out_banks[j // 2]
                        out = ob.view[:, (j % 2) * D:(j % 2 + 1) * D]
                        for part in (hh, hl):
                            first = block == 0 and part is hh and j % 2 == 0
                            last = block == w.hidden_blocks - 1 and part is hl
                            done = core.pe.do(lambda e, j=j, block=block, part=part, out=out, first=first, last=last: e.matmul(
                                out, part.view[:, j * P:(j + 1) * P], w.sign2[:, block, :],
                                start=first, stop=last, skip_group_check=True),
                                ready_h, *(ob.free if block == 0 else []), signal=(j == GT - 1 and part is hl))
                    hh.free = [done]
            emptied.append((g, done))

        emptied = []

        scaled = []

        def scale_output():
            g, done = emptied.pop(0)
            g_out = g_ring.take()
            for half_bank, ob in enumerate(out_banks):
                view = g_out.view[:, 2 * half_bank:2 * half_bank + 2, :]
                psum = ob.view.rearrange("p (t d) -> p t d", t=2)
                t = core.dve.do(lambda e, view=view, psum=psum: e.tensor_tensor(
                    view, psum, w.alpha2[:, :].unsqueeze(1).broadcast_to([P, 2, D]), ALU.mult), done, *g_out.free)
                ob.free = [t]
                t = core.dve.do(lambda e, view=view: e.tensor_tensor(
                    view, view, w.b2[:, :].unsqueeze(1).broadcast_to([P, 2, D]), ALU.add), t)
            scaled.append((g, g_out, t))

        def gate_to_dram():
            g, g_out, t = scaled.pop(0)
            t = core.act.do(lambda e: e.activation(g_out.view[:, :, :], g_out.view[:, :, :], ACT.Silu), t)
            rows = g_dram[(b * GROUPS + g) * GROUP:(b * GROUPS + g + 1) * GROUP, :]
            g_out.free = [core.sp.dma(g_out.dma_sem, lambda e: e.dma_start(
                rows.rearrange("(j p) d -> p j d", p=P), g_out.view[:, :, :]), t)]

        ready = finish(load_group(0))
        for g in range(GROUPS):
            ahead = load_group(g + 1) if g + 1 < GROUPS else None
            ready = merge(group(g, ready), ahead)
        scale_output()
        gate_to_dram()
        core.hand_over()


def finish(thread):
    while True:
        try:
            next(thread)
        except StopIteration as e:
            return e.value


def merge(main, ahead):
    result = None
    for _ in main:
        if ahead is not None:
            try:
                next(ahead)
            except StopIteration as e:
                result, ahead = e.value, None
    if ahead is not None:
        result = finish(ahead)
    return result


class Layer0Weights:

    def __init__(self, core, ctx, consts, a):
        self.hidden_blocks = a["w1T"].shape[1] // P
        hb = self.hidden_blocks
        hidden = hb * P
        self.qkv_16 = core.sb(ctx, "qkv_16", [P, 3 * D], F16)
        self.qkv_hi = core.sb(ctx, "qkv_hi", [P, 3 * D], F32R)
        self.qkv_lo = core.sb(ctx, "qkv_lo", [P, 3 * D], F32R)
        self.sign1 = core.sb(ctx, "sign1", [P, DC, hidden], F32R)
        self.sign2 = core.sb(ctx, "sign2", [P, hb, D], F32R)
        self.alpha1 = core.sb(ctx, "alpha1", [P, hb], F32)
        self.b1 = core.sb(ctx, "b1", [P, hb], F32)
        self.alpha2 = core.sb(ctx, "alpha2", [P, D], F32)
        self.b2 = core.sb(ctx, "b2", [P, D], F32)
        self.wo_hi = core.sb(ctx, "wo_hi", [P, DC, D], F32R)
        self.wo_lo = core.sb(ctx, "wo_lo", [P, DC, D], F32R)
        self.out_b = core.sb(ctx, "out_b", [P, D], F32)
        vecs = DmaSem(core, "layer0_vectors_dma")
        core.sp.dma(vecs, lambda e: e.dma_start(self.b1[:, :], a["b1"].rearrange("(f p) -> p f", p=P), allow_slow_non_contiguous=True))
        core.sp.dma(vecs, lambda e: e.dma_start(self.b2[:, :], a["b2"].partition_broadcast(P)))
        loaded = core.sp.dma(vecs, lambda e: e.dma_start(self.out_b[:, :], a["out_b"].partition_broadcast(P)))
        with ExitStack() as tmp:
            bank = tmp.enter_context(core.nc.psum_tensor("alpha2_bank", [P, BANK], F32))
            stage = core.dma_ring(tmp, "layer0_stage", 4, [P, 2048], F32)
            mask = core.sb(tmp, "negative", [P, 2048], F32)
            alpha2_col = core.sb(tmp, "alpha2_col", [P, DC], F32)
            alpha2_wide = core.sb(tmp, "alpha2_wide", [P, DC, P], F32)
            dve = core.dve

            def load(dram, shape):
                s = stage.take()
                n = shape[0] * shape[1]
                view = s.view[:, 0:n].rearrange("p (a n) -> p a n", a=shape[0])
                return s, view, core.sp.dma(s.dma_sem, lambda e: e.dma_start(view, dram), *s.free)

            s, v, t = load(a["qkv"].rearrange("(c p) n -> p c n", p=P), (DC, 3 * D))
            dve.do(lambda e, v=v: e.tensor_copy(self.qkv_16[:, :], v[:, 0, :]), t)
            s.free = [split_weights(core, v[:, 1, :], self.qkv_hi[:, :], self.qkv_lo[:, :], t)]
            s, v, t = load(a["w1"].rearrange("(f p) d -> p f d", p=P), (hb, D))
            u = dve.do(lambda e, v=v: e.tensor_reduce(self.alpha1[:, :], v, AX_X, ALU.add, apply_absolute_value=True), t)
            s.free = [u]
            dve.do(lambda e: e.tensor_scalar(self.alpha1[:, :], self.alpha1[:, :], 1.0 / D, None, ALU.mult), u)
            s, v, t = load(a["w2"].rearrange("(c p) h -> p c h", p=P), (DC, hidden))
            u = dve.do(lambda e, v=v: e.tensor_reduce(alpha2_col[:, :], v, AX_X, ALU.add, apply_absolute_value=True), t)
            s.free = [u]
            for c in range(DC):
                u2 = dve.do(lambda e, c=c: e.tensor_scalar(
                    alpha2_wide[:, c, :], consts.ones[:, :], alpha2_col[:, c:c + 1], 1.0 / hidden, ALU.mult, ALU.mult),
                    u, consts.ready)
            for c in range(DC):
                m = core.pe.do(lambda e, c=c: e.matmul(bank[:, c * P:(c + 1) * P], alpha2_wide[:, c, :], consts.identity[:, :],
                                                       start=True, stop=True), u2, consts.ready)
            dve.do(lambda e: e.tensor_copy(self.alpha2[:, :], bank[:, 0:D]), m)
            masked = None
            for dram, shape, out in (
                (a["w1T"].rearrange("(c p) h -> p c h", p=P), (DC, hidden), self.sign1),
                (a["w2T"].rearrange("(f p) d -> p f d", p=P), (hb, D), self.sign2),
            ):
                s, v, t = load(dram, shape)
                m = mask[:, 0:shape[0] * shape[1]].rearrange("p (a n) -> p a n", a=shape[0])
                u = dve.do(lambda e, v=v, m=m: e.tensor_scalar(m, v, 0.0, None, ALU.is_lt), t, masked)
                masked = dve.do(lambda e, v=v, m=m, out=out: e.scalar_tensor_tensor(
                    out[:, :, :], v, 0.0, m, ALU.is_gt, ALU.subtract), u)
                s.free = [masked]
            s, v, t = load(a["woT"].rearrange("(c p) n -> p c n", p=P), (DC, D))
            self.ready = split_weights(core, v, self.wo_hi[:, :, :], self.wo_lo[:, :, :], t, loaded)
            s.free = [self.ready]
            core.hand_over()


class KeysValues:

    def __init__(self, core, ctx):
        self.k_hi = core.sb(ctx, "k_hi", [P, DC, SEQ], F32R)
        self.k_lo = core.sb(ctx, "k_lo", [P, DC, SEQ], F32R)
        self.v = core.sb(ctx, "v_hi_lo", [P, SEQ // P, 2 * D], F32R)


KEYS = 1024
KEY_CHUNKS = SEQ // KEYS
KEY_BLOCKS = KEYS // P


def attention(core, consts, w, kv, b, x_dram, q_dram, g_dram, x1_dram, xn1_dram):
    pe, act, dve, pool, sp = core.lanes
    with ExitStack() as ctx:
        banks_s = [ctx.enter_context(core.nc.psum_tensor(f"scores{b}_{i}", [P, KEYS], F32)) for i in range(2)]
        s_ring = Ring([Slot(t) for t in banks_s])
        pt_ring = Ring([Slot(ctx.enter_context(core.nc.psum_tensor(f"pt{b}_{i}", [P, BANK], F32))) for i in range(2)])
        y_bank = Slot(ctx.enter_context(core.nc.psum_tensor(f"ybank{b}", [P, 2 * D], F32)))
        misc = Slot(ctx.enter_context(core.nc.psum_tensor(f"misc{b}", [P, BANK], F32)))
        q_raw = core.dma_ring(ctx, f"q_raw_b{b}_", 1, [P, DC, GROUP], F32)
        q_hi = core.ring(ctx, f"q_hi_b{b}_", 2, [P, DC, GROUP], F32R)
        q_lo = core.ring(ctx, f"q_lo_b{b}_", 2, [P, DC, GROUP], F32R)
        p_ring = core.ring(ctx, f"p_b{b}_", 2, [P, KEYS], F32)
        pt_hi = core.ring(ctx, f"pt_hi_b{b}_", 2, [P, BANK], F32R)
        pt_lo = core.ring(ctx, f"pt_lo_b{b}_", 2, [P, BANK], F32R)
        acc_ring = core.ring(ctx, f"acc_b{b}_", 2, [P, D], F32)
        col_ring = core.ring(ctx, f"softmax_cols_b{b}_", 2, [P, 5, KEY_CHUNKS + 1], F32)
        yt_hi = core.sb(ctx, f"yt_hi_b{b}", [P, DC, P], F32R)
        yt_lo = core.sb(ctx, f"yt_lo_b{b}", [P, DC, P], F32R)
        x_ring = core.dma_ring(ctx, f"x_res_b{b}_", 2, [P, D], F32)
        g_ring = core.dma_ring(ctx, f"g_in_b{b}_", 2, [P, D], F32)
        xn_ring = core.dma_ring(ctx, f"xn1_out_b{b}_", 1, [P, D], F32)
        norm = LayerNorm(core, ctx, consts, f"ln1_b{b}", 1)
        tiles = SEQ // P
        steps = [(t, c) for t in range(tiles) for c in range(KEY_CHUNKS)]
        state = {}
        yt_free = [None]

        def queries(group):
            raw, hi, lo = q_raw.take(), q_hi.take(), q_lo.take()
            t = sp.dma(raw.dma_sem, lambda e: e.dma_start(raw.view[:, :, :], q_dram[b * GROUPS + group]), *raw.free)
            th = dve.do(lambda e: e.tensor_copy(hi.view[:, :, :], raw.view[:, :, :]), t, *hi.free)
            tl = dve.do(lambda e: e.tensor_tensor(lo.view[:, :, :], raw.view[:, :, :], f32(hi.view[:, :, :]), ALU.subtract), th)
            raw.free = [tl]
            return hi, lo, tl

        def scores(i, half):
            t, c = steps[i]
            if half == 0:
                slot = s_ring.take()
                state[i] = {"s": slot}
            slot = state[i]["s"]
            hi, lo, ready = state["q", t // GT]
            rows = slice((t % GT) * P, (t % GT + 1) * P)
            keys = slice(c * KEYS + half * BANK, c * KEYS + (half + 1) * BANK)
            out = slot.view[:, half * BANK:(half + 1) * BANK]
            for n, (d, qs, ks) in enumerate([(d, qs, ks) for d in range(DC) for qs, ks in ((hi, kv.k_hi), (hi, kv.k_lo), (lo, kv.k_hi))]):
                done = pe.do(lambda e, n=n, d=d, qs=qs, ks=ks: e.matmul(out, qs.view[:, d, rows], ks[:, d, keys],
                                                                       start=(n == 0), stop=(n == 3 * DC - 1)),
                             ready, *slot.free, signal=(n == 3 * DC - 1))
            state[i]["scored"] = done
            if c == KEY_CHUNKS - 1 and half == 1 and t % GT == GT - 1:
                hi.free = [done]

        def running_max(i):
            t, c = steps[i]
            st = state[i]
            if c == 0:
                state["cols", t] = col_ring.take()
            cols = state["cols", t]
            v = cols.view
            free = cols.free if c == 0 else []
            slot = st["s"]
            m = dve.do(lambda e: e.tensor_reduce(v[:, 0, c:c + 1], slot.view[:, :], AX_X, ALU.max, negate=True), st["scored"], *free)
            if c == 0:
                m = dve.do(lambda e: e.tensor_copy(v[:, 1, 0:1], v[:, 0, 0:1]), m)
            else:
                m = dve.do(lambda e: e.tensor_tensor(v[:, 1, c:c + 1], v[:, 1, c - 1:c], v[:, 0, c:c + 1], ALU.min), m)
            st["max"] = m

        def exponentials(i):
            t, c = steps[i]
            st = state[i]
            v = state["cols", t].view
            p = p_ring.take()
            st["p"] = p
            slot = st["s"]
            st["exp"] = act.do(lambda e: e.activation(p.view[:, :], slot.view[:, :], ACT.Exp, bias=v[:, 1, c:c + 1],
                                                      accum_out=v[:, 3, c:c + 1]), st["max"], *p.free)
            slot.free = [st["exp"]]
            if c:
                st["corr"] = act.do(lambda e: e.activation(v[:, 2, c:c + 1], v[:, 1, c - 1:c], ACT.Exp, bias=v[:, 1, c:c + 1], scale=-1.0))

        def turn(i, half):
            st = state[i]
            bank, hi, lo = pt_ring.take(), pt_hi.take(), pt_lo.take()
            for k in range(4):
                kb = 4 * half + k
                done = pe.do(lambda e, k=k, kb=kb: e.transpose(bank.view[:, k * P:(k + 1) * P], st["p"].view[:, kb * P:(kb + 1) * P],
                                                               consts.identity[:, :]), st["exp"], *bank.free, signal=(k == 3))
            if half == 1:
                st["p"].free = [done]
            th = act.do(lambda e: e.activation(hi.view[:, :], bank.view[:, :], ACT.Copy), done, *hi.free)
            tl = dve.do(lambda e: e.tensor_tensor(lo.view[:, :], bank.view[:, :], f32(hi.view[:, :]), ALU.subtract), th, *hi.free)
            bank.free = [tl]
            st["pt", half] = (hi, lo, tl)

        def values(i, half):
            t, c = steps[i]
            st = state[i]
            hi, lo, ready = st["pt", half]
            for k in range(4):
                kb = 4 * half + k
                block = c * KEY_BLOCKS + kb
                pe.do(lambda e, k=k, kb=kb, block=block: e.matmul(y_bank.view[:, :], hi.view[:, k * P:(k + 1) * P], kv.v[:, block, :],
                                                                  start=(kb == 0), stop=False, skip_group_check=True),
                      ready, *y_bank.free, signal=False)
                done = pe.do(lambda e, k=k, kb=kb, block=block: e.matmul(y_bank.view[:, 0:D], lo.view[:, k * P:(k + 1) * P], kv.v[:, block, 0:D],
                                                                        start=False, stop=(kb == KEY_BLOCKS - 1), skip_group_check=True),
                             signal=(k == 3))
            hi.free = [done]
            st["pv"] = done

        def accumulate(i):
            t, c = steps[i]
            st = state[i]
            v = state["cols", t].view
            if c == 0:
                state["acc", t] = acc_ring.take()
                acc = state["acc", t]
                a = dve.do(lambda e: e.tensor_copy(acc.view[:, :], y_bank.view[:, 0:D]), st["pv"], *acc.free)
                l = dve.do(lambda e: e.tensor_copy(v[:, 4, 0:1], v[:, 3, 0:1]), st["exp"])
            else:
                acc = state["acc", t]
                a = dve.do(lambda e: e.scalar_tensor_tensor(acc.view[:, :], acc.view[:, :], v[:, 2, c:c + 1], y_bank.view[:, 0:D],
                                                            ALU.mult, ALU.add), st["pv"], st["corr"], state["acc_done", t])
                l = dve.do(lambda e: e.scalar_tensor_tensor(v[:, 4, c:c + 1], v[:, 4, c - 1:c], v[:, 2, c:c + 1], v[:, 3, c:c + 1],
                                                            ALU.mult, ALU.add), state["sum_done", t])
            a = dve.do(lambda e: e.tensor_tensor(acc.view[:, :], acc.view[:, :], y_bank.view[:, D:2 * D], ALU.add), a)
            y_bank.free = [a]
            state["acc_done", t], state["sum_done", t] = a, l

        def residual(t):
            acc, cols = state["acc", t], state["cols", t]
            v = cols.view
            row = (b * SEQ + t * P, b * SEQ + (t + 1) * P)
            xs, gs = x_ring.take(), g_ring.take()
            x_in = sp.dma(xs.dma_sem, lambda e: e.dma_start(xs.view[:, :], x_dram[row[0]:row[1], :]), *xs.free)
            g_in = sp.dma(gs.dma_sem, lambda e: e.dma_start(gs.view[:, :], g_dram[row[0]:row[1], :]), *gs.free)
            tr = dve.do(lambda e: e.reciprocal(v[:, 0, KEY_CHUNKS:KEY_CHUNKS + 1], v[:, 4, KEY_CHUNKS - 1:KEY_CHUNKS]), state["sum_done", t])
            ty = dve.do(lambda e: e.tensor_scalar(acc.view[:, :], acc.view[:, :], v[:, 0, KEY_CHUNKS:KEY_CHUNKS + 1], None, ALU.mult), tr)
            cols.free = [ty]
            yield
            for c in range(DC):
                done = pe.do(lambda e, c=c: e.transpose(misc.view[:, c * P:(c + 1) * P], acc.view[:, c * P:(c + 1) * P], consts.identity[:, :]),
                             ty, *misc.free, signal=(c == DC - 1))
            acc.free = [done]
            pair = misc.view[:, 0:D].rearrange("p (c q) -> p c q", c=DC)
            split = split_from_psum(core, pair, yt_hi[:, :, :], yt_lo[:, :, :], done, yt_free[0])
            yield
            out = misc.view[:, D:2 * D]
            for n, (c, ys, ws) in enumerate([(c, ys, ws) for c in range(DC) for ys, ws in ((yt_hi, w.wo_hi), (yt_hi, w.wo_lo), (yt_lo, w.wo_hi))]):
                done = pe.do(lambda e, n=n, c=c, ys=ys, ws=ws: e.matmul(out, ys[:, c, :], ws[:, c, :], start=(n == 0), stop=(n == 3 * DC - 1)),
                             split, signal=(n == 3 * DC - 1))
            yt_free[0] = done
            ts = dve.do(lambda e: e.tensor_tensor(acc.view[:, :], out, w.out_b[:, :], ALU.add), done)
            misc.free = [ts]
            ts = pool.do(lambda e: e.tensor_tensor(acc.view[:, :], acc.view[:, :], gs.view[:, :], ALU.mult), ts, g_in)
            gs.free = [ts]
            ts = pool.do(lambda e: e.tensor_tensor(xs.view[:, :], xs.view[:, :], acc.view[:, :], ALU.add), ts, x_in)
            acc.free = [ts]
            saved = sp.dma(xs.dma_sem, lambda e: e.dma_start(x1_dram[row[0]:row[1], :], xs.view[:, :]), ts)
            yield
            xn = xn_ring.take()
            tn = norm([xs.view[:, :]], [xn.view[:, :]], ts, *xn.free)
            xs.free = [saved, tn]
            xn.free = [sp.dma(xn.dma_sem, lambda e: e.dma_start(xn1_dram[row[0]:row[1], :], xn.view[:, :]), tn)]

        state["q", 0] = queries(0)
        scores(0, 0)
        scores(0, 1)
        running_max(0)
        exponentials(0)
        pending = None
        for i, (t, c) in enumerate(steps):
            more = i + 1 < len(steps)
            if c == 1 and t % GT == 2 and t // GT + 1 < tiles // GT:
                state["q", t // GT + 1] = queries(t // GT + 1)
            if more:
                scores(i + 1, 0)
            turn(i, 0)
            if more:
                scores(i + 1, 1)
            turn(i, 1)
            if more:
                running_max(i + 1)
                exponentials(i + 1)
            values(i, 0)
            if pending is not None:
                next(pending, None)
            values(i, 1)
            accumulate(i)
            state.pop(i)
            if c == KEY_CHUNKS - 1:
                if pending is not None:
                    finish(pending)
                pending = residual(t)
        finish(pending)
        core.hand_over()
CHUNK = 512
CHUNKS = SEQ // CHUNK
INNER = 128
STATES = 64
PAIR = 2
PAIRS = STATES // PAIR
AHEAD = 2
LAG = 4

EXPERTS = 16
CAPACITY = 2 * SEQ // EXPERTS
LISTS = BATCH * EXPERTS
TILES = SEQ // P
SLOT_TILES = CAPACITY // P
HIDDEN = 512
HB = HIDDEN // P
COLS32 = 32
ROWS16 = CAPACITY // COLS32
SCORE_BITS = 30
SHARED_RATE = 0.98
CHOOSE_RATE = 1.3
EXPERTS_RATE = 0.98


class ScanWeights:

    def __init__(self, core, ctx, consts, a):
        sb = core.sb
        self.up_hi = sb(ctx, "up_hi", [P, DC, D], F32R)
        self.up_lo = sb(ctx, "up_lo", [P, DC, D], F32R)
        self.delta_hi = sb(ctx, "wdelta_hi", [P, INNER], F32R)
        self.delta_lo = sb(ctx, "wdelta_lo", [P, INNER], F32R)
        self.bc_hi = sb(ctx, "bc_hi", [P, 2, P], F32R)
        self.bc_lo = sb(ctx, "bc_lo", [P, 2, P], F32R)
        self.down_hi = sb(ctx, "down_hi", [P, D], F32R)
        self.down_lo = sb(ctx, "down_lo", [P, D], F32R)
        self.b_down = sb(ctx, "b_down", [P, D], F32)
        self.gamma = sb(ctx, "gamma", [P, DC], F32)
        self.beta = sb(ctx, "beta", [P, DC], F32)
        self.b_up = sb(ctx, "b_up", [P, DC], F32)
        self.conv_w = sb(ctx, "conv_w", [P, 3], F32)
        self.conv_b = sb(ctx, "conv_b", [P, 1], F32)
        self.b_delta = sb(ctx, "b_delta", [P, 1], F32)
        self.skip = sb(ctx, "skip", [P, 1], F32)
        self.a = sb(ctx, "a_neg", [P, STATES], F32)
        self.select = sb(ctx, "select_state", [P, STATES], F32R)
        vecs = DmaSem(core, "scan_vectors_dma")
        col = lambda ap: ap.rearrange("(c p) -> p c", p=P)
        for dst, src in ((self.gamma, col(a["ln_gamma"])), (self.beta, col(a["ln_beta"])), (self.b_up, col(a["b_up"])),
                         (self.conv_w, a["conv_w"]), (self.conv_b, col(a["conv_b"])), (self.b_delta, col(a["b_delta"])),
                         (self.skip, col(a["D"])), (self.a, a["A_log"]), (self.b_down, a["b_down"].partition_broadcast(P))):
            vt = core.sp.dma(vecs, lambda e, dst=dst, src=src: e.dma_start(dst[:, :], src, allow_slow_non_contiguous=True))
        t = core.act.do(lambda e: e.activation(self.a[:, :], self.a[:, :], ACT.Exp), vt)
        core.dve.do(lambda e: e.tensor_scalar(self.a[:, :], self.a[:, :], -1.0, None, ALU.mult), t)
        with ExitStack() as tmp:
            stage = DmaSem(core, "scan_stage_dma")
            up = core.sb(tmp, "up_raw", [P, DC, D], F32)
            delta = core.sb(tmp, "wdelta_raw", [P, INNER], F32)
            bc = core.sb(tmp, "bc_raw", [P, 2, 2, STATES], F32)
            down = core.sb(tmp, "down_raw", [P, D], F32)
            sel = core.sb(tmp, "select_raw", [P, STATES], F32)
            core.sp.dma(stage, lambda e: e.dma_start(up[:, :, :], a["W_up"].rearrange("(c p) n -> p c n", p=P)))
            core.sp.dma(stage, lambda e: e.dma_start(delta[:, :], a["W_delta"]))
            for m, name in enumerate(("W_B", "W_C")):
                for twice in range(2):
                    core.sp.dma(stage, lambda e, m=m, name=name, twice=twice: e.dma_start(bc[:, m, twice, :], a[name]))
            t = core.sp.dma(stage, lambda e: e.dma_start(down[:, :], a["W_down"]))
            split_weights(core, up[:, :, :], self.up_hi[:, :, :], self.up_lo[:, :, :], t)
            split_weights(core, delta[:, :], self.delta_hi[:, :], self.delta_lo[:, :])
            split_weights(core, bc[:, :, :, :].rearrange("p m t n -> p m (t n)"), self.bc_hi[:, :, :], self.bc_lo[:, :, :])
            split_weights(core, down[:, :], self.down_hi[:, :], self.down_lo[:, :])
            t = core.pool.do(lambda e: e.memset(sel[:, :], 0.0))
            for half in range(2):
                t = core.pool.do(lambda e, half=half: e.affine_select(
                    out=sel[:, :], in_=sel[:, :], compare_op=ALU.not_equal, fill=1.0,
                    base=-STATES * half, pattern=[[-1, STATES]], channel_multiplier=1), t)
            core.dve.do(lambda e: e.tensor_copy(self.select[:, :], sel[:, :]), t)
            core.hand_over()


class SelectiveScan:

    def __init__(self, core, ctx, consts, w, banks, pair_banks, xn_dram, s_dram):
        self.core, self.consts, self.w, self.xn_dram, self.s_dram = core, consts, w, xn_dram, s_dram
        ring = lambda name, n, shape=(P, CHUNK), dt=F32: core.ring(ctx, name, n, list(shape), dt)
        pair = (P, PAIR, CHUNK)
        self.b_bank = Slot(pair_banks[0][:, :, :])
        self.c_bank = Slot(pair_banks[1][:, :, :])
        self.y_bank = Slot(banks[0][:, :])
        self.bank = Slot(banks[1][:, :])
        self.xn = core.dma_ring(ctx, "scan_xn", 1, [P, GT, D], F32)
        self.yt_hi = core.sb(ctx, "scan_yt_hi", [P, DC, CHUNK], F32R)
        self.yt_lo = core.sb(ctx, "scan_yt_lo", [P, DC, CHUNK], F32R)
        self.yt_free = None
        self.left = core.sb(ctx, "scan_left", [P, 2 + CHUNK], F32)
        self.left_free = None
        self.gate = ring("scan_gate", 2)
        self.temp = ring("scan_temp", 4)
        self.u = ring("scan_u", 2)
        self.u_hi = ring("scan_u_hi", 1, dt=F32R)
        self.u_lo = ring("scan_u_lo", 1, dt=F32R)
        self.delta = ring("scan_delta", 2)
        self.du = ring("scan_du", 2)
        self.bb = ring("scan_bb", 2, dt=F32R)
        self.cc = ring("scan_cc", 2, dt=F32R)
        self.out = core.dma_ring(ctx, "scan_out", 2, [P, 2, D], F32)
        self.decay = ring("scan_decay", AHEAD + 1, pair)
        self.drive = ring("scan_drive", 2, pair)
        self.h = ring("scan_h", 2, pair)
        self.ch = ring("scan_ch", 2, pair)
        self.ch_sum = ring("scan_ch_sum", LAG)
        self.state = core.sb(ctx, "scan_state", [P, STATES], F32)
        self.state_free = {}
        self.norm = LayerNorm(core, ctx, consts, "ln_scan", 1)

    def prepare(self, chunk):
        core, w, consts = self.core, self.w, self.consts
        pe, act, dve, pool, sp = core.lanes
        st = {}
        xs = self.xn.take()
        rows = self.xn_dram[chunk * CHUNK:(chunk + 1) * CHUNK, :]
        loaded = sp.dma(xs.dma_sem, lambda e: e.dma_start(xs.view[:, :, :], rows.rearrange("(j p) d -> p j d", p=P)), *xs.free)
        yield
        tiles = [xs.view[:, j, :] for j in range(GT)]
        for _ in range(4):
            yield
        measured = self.norm.statistics(tiles, loaded)
        yield
        yield
        normed = self.norm.apply(measured, tiles, tiles)
        bank = self.bank
        for c in range(DC):
            yield
            for j in range(GT):
                done = pe.do(lambda e, j=j, c=c: e.transpose(bank.view[:, j * P:(j + 1) * P], xs.view[:, j, c * P:(c + 1) * P], consts.identity[:, :]),
                             normed, *bank.free, signal=(j == GT - 1))
            yt = self.temp.take()
            t = act.do(lambda e, c=c, yt=yt: e.activation(yt.view[:, :], bank.view, ACT.Identity, bias=w.beta[:, c:c + 1], scale=w.gamma[:, c:c + 1]),
                       done, *yt.free)
            bank.free = [t]
            split = split_weights_on_pool(core, yt.view[:, :], self.yt_hi[:, c, :], self.yt_lo[:, c, :], t, self.yt_free)
            yt.free = [split]
        yield
        xs.free = [done]

        def project(cols):
            parts = [(c, ws, ys) for c in range(DC) for ws, ys in ((w.up_hi, self.yt_hi), (w.up_hi, self.yt_lo), (w.up_lo, self.yt_hi))]
            for n, (c, ws, ys) in enumerate(parts):
                done = pe.do(lambda e, n=n, c=c, ws=ws, ys=ys: e.matmul(bank.view, ws[:, c, cols], ys[:, c, :], start=(n == 0), stop=(n == len(parts) - 1)),
                             split, *bank.free, signal=(n == len(parts) - 1))
            return done

        yield
        if chunk % CHUNKS == 0:
            t = dve.do(lambda e: e.memset(self.left[:, 0:2], 0.0), self.left_free)
        else:
            t = dve.do(lambda e: e.tensor_copy(self.left[:, 0:2], self.left[:, CHUNK:CHUNK + 2]), self.left_free)
        done = project(slice(0, INNER))
        left_in = act.do(lambda e: e.activation(self.left[:, 2:2 + CHUNK], bank.view, ACT.Identity, bias=w.b_up[:, 0:1]), done, t)
        bank.free = [left_in]
        yield
        conv = self.temp.take()
        t = dve.do(lambda e: e.tensor_scalar(conv.view[:, :], self.left[:, 0:CHUNK], w.conv_w[:, 0:1], w.conv_b[:, 0:1], ALU.mult, ALU.add),
                   left_in, *conv.free)
        for k in (1, 2):
            t = dve.do(lambda e, k=k: e.scalar_tensor_tensor(conv.view[:, :], self.left[:, k:k + CHUNK], w.conv_w[:, k:k + 1], conv.view[:, :],
                                                             ALU.mult, ALU.add), t)
        self.left_free = t
        done = project(slice(INNER, 2 * INNER))
        self.yt_free = done
        yield
        gate, u = self.gate.take(), self.u.take()
        gated = act.do(lambda e: e.activation(gate.view[:, :], bank.view, ACT.Silu, bias=w.b_up[:, 1:2]), done, *gate.free)
        bank.free = [gated]
        st["gate"], st["gate_ready"] = gate, gated
        u_hi, u_lo = self.u_hi.take(), self.u_lo.take()
        t = act.do(lambda e: e.activation(u.view[:, :], conv.view[:, :], ACT.Silu), t, *u.free)
        conv.free = [t]
        st["u"], u_ready = u, t
        split = split_weights_on_pool(core, u.view[:, :], u_hi.view[:, :], u_lo.view[:, :], t, *u_hi.free)
        for _ in range(4):
            yield

        def from_u(hi, lo):
            for n, (ws, us) in enumerate(((hi, u_hi), (hi, u_lo), (lo, u_hi))):
                done = pe.do(lambda e, n=n, ws=ws, us=us: e.matmul(bank.view, ws, us.view[:, :], start=(n == 0), stop=(n == 2)),
                             split, *bank.free, signal=(n == 2))
            return done

        done = from_u(w.delta_hi[:, :], w.delta_lo[:, :])
        x, z, one_z, log = (self.temp.take() for _ in range(4))
        delta, du = self.delta.take(), self.du.take()
        v = lambda s: s.view[:, :]
        x_in = act.do(lambda e: e.activation(v(x), bank.view, ACT.Identity, bias=w.b_delta[:, 0:1]), done, *x.free)
        bank.free = [x_in]
        for _ in range(3):
            yield
        t = dve.do(lambda e: e.scalar_tensor_tensor(v(z), v(x), -1.0, v(x), ALU.mult, ALU.min), x_in, *z.free)
        yield
        z_in = act.do(lambda e: e.activation(v(z), v(z), ACT.Exp), t)
        t = pool.do(lambda e: e.tensor_scalar(v(one_z), v(z), 1.0, 1.0, ALU.mult, ALU.add), z_in, *one_z.free)
        yield
        logged = act.do(lambda e: e.activation(v(log), v(one_z), ACT.Ln), t, *log.free)
        t = pool.do(lambda e: e.tensor_scalar(v(one_z), v(one_z), 1.0, -1.0, ALU.mult, ALU.add), logged)
        rest = pool.do(lambda e: e.tensor_tensor(v(z), v(z), v(one_z), ALU.subtract), t)
        yield
        t = act.do(lambda e: e.activation(v(one_z), v(log), ACT.Exp, scale=-1.0), logged, rest)
        t = pool.do(lambda e: e.tensor_tensor(v(z), v(z), v(one_z), ALU.mult), t)
        one_z.free = [t]
        t = pool.do(lambda e: e.tensor_tensor(v(log), v(log), v(z), ALU.add), t)
        z.free = [t]
        yield
        yield
        yield
        delta_in = dve.do(lambda e: e.scalar_tensor_tensor(v(delta), v(x), 0.0, v(log), ALU.max, ALU.add), t, *delta.free)
        x.free, log.free = [delta_in], [delta_in]
        yield
        du_in = pool.do(lambda e: e.tensor_tensor(v(du), v(delta), v(u), ALU.mult), delta_in, u_ready, *du.free)
        st["delta"], st["delta_ready"], st["du"], st["du_ready"] = delta, delta_in, du, du_in
        for m, (name, r) in enumerate((("bb", self.bb), ("cc", self.cc))):
            yield
            s = r.take()
            done = from_u(w.bc_hi[:, m, :], w.bc_lo[:, m, :])
            t = act.do(lambda e, s=s: e.activation(s.view[:, :], bank.view, ACT.Copy), done, *s.free)
            yield
            yield
            yield
            t = dve.do(lambda e, s=s: e.tensor_tensor(s.view[STATES:P, :], bank.view[STATES:P, :], f32(s.view[STATES:P, :]), ALU.subtract), t)
            bank.free = [t]
            st[name], st[name + "_ready"] = s, t
        u_hi.free = [done]
        return st

    def load_residual(self, chunk, st):
        st["outs"] = []
        for pair in range(GT // 2):
            o = self.out.take()
            rows = chunk * CHUNK + pair * 2 * P
            loaded = self.core.sp.dma(o.dma_sem, lambda e, rows=rows, o=o: e.dma_start(
                o.view[:, :, :], self.xn_dram[rows:rows + 2 * P, :].rearrange("(j p) d -> p j d", p=P)), *o.free)
            st["outs"].append((o, rows, loaded))

    def finish_chunk(self, chunk, st):
        core, w = self.core, self.w
        pe, act, dve, pool, sp = core.lanes
        y, g_hi, g_lo = self.temp.take(), self.u_hi.take(), self.u_lo.take()
        u, gate = st["u"], st["gate"]
        outs = st["outs"]
        t = dve.do(lambda e: e.scalar_tensor_tensor(y.view[:, :], u.view[:, :], w.skip[:, 0:1], self.y_bank.view, ALU.mult, ALU.add),
                   st["y_done"], *y.free)
        self.y_bank.free, u.free = [t], [t]
        yield
        t = pool.do(lambda e: e.tensor_tensor(y.view[:, :], y.view[:, :], gate.view[:, :], ALU.mult), t, st["gate_ready"])
        gate.free = [t]
        split = split_weights_on_pool(core, y.view[:, :], g_hi.view[:, :], g_lo.view[:, :], t, *g_hi.free)
        y.free = [split]
        bank = self.bank
        yield
        yield
        for pair in range(GT // 2):
            yield
            for k in range(2):
                j = 2 * pair + k
                rows = slice(j * P, (j + 1) * P)
                out = bank.view[:, k * D:(k + 1) * D]
                for n, (gs, ws) in enumerate(((g_hi, w.down_hi), (g_hi, w.down_lo), (g_lo, w.down_hi))):
                    done = pe.do(lambda e, n=n, gs=gs, ws=ws, rows=rows, out=out: e.matmul(out, gs.view[:, rows], ws[:, :], start=(n == 0), stop=(n == 2)),
                                 split, *bank.free, signal=(n == 2 and k == 1))
            yield
            o, rows, residual = outs[pair]
            psum = bank.view.rearrange("p (t d) -> p t d", t=2)
            t = dve.do(lambda e, o=o, psum=psum: e.tensor_tensor(o.view[:, :, :], psum, o.view[:, :, :], ALU.add), done, residual)
            bank.free = [t]
            t = pool.do(lambda e, o=o: e.tensor_tensor(o.view[:, :, :], o.view[:, :, :], w.b_down[:, :].unsqueeze(1).broadcast_to([P, 2, D]), ALU.add), t)
            o.free = [sp.dma(o.dma_sem, lambda e, rows=rows, o=o: e.dma_start(
                self.s_dram[rows:rows + 2 * P, :].rearrange("(j p) d -> p j d", p=P), o.view[:, :, :]), t)]
        g_hi.free = [done]

    def thread(self):
        core, w = self.core, self.w
        pe, act, dve, pool, sp = core.lanes
        items = [(k, m) for k in range(BATCH * CHUNKS) for m in range(PAIRS)]
        chunks = {0: (yield from self.prepare(0))}
        work = {}
        helpers = []

        def broadcast(i, what, s):
            k, m = items[i]
            st = chunks[k]
            src = st[what]
            work.setdefault(i, {})
            for j in range(PAIR):
                n = m * PAIR + j
                work[i][what + "_done"] = pe.do(lambda e, j=j, n=n: e.matmul(s.view[:, j, :], w.select[:, n:n + 1].broadcast_to([P, P]), src.view[:, :],
                                                                            start=True, stop=True),
                                                st[what + "_ready"], *s.free, signal=(j == PAIR - 1))
            if m == PAIRS - 1:
                src.free = [work[i][what + "_done"]]

        def decay(i):
            k, m = items[i]
            st, it = chunks[k], work.setdefault(i, {})
            s = self.decay.take()
            it["decay"] = s
            for j in range(PAIR):
                n = m * PAIR + j
                it["decay_done"] = act.do(lambda e, j=j, n=n: e.activation(s.view[:, j, :], st["delta"].view[:, :], ACT.Exp, scale=w.a[:, n:n + 1]),
                                          st["delta_ready"], *s.free, signal=(j == PAIR - 1))
            if m == PAIRS - 1:
                st["delta"].free = [it["decay_done"]]

        def drive(i):
            k, m = items[i]
            st, it = chunks[k], work[i]
            s = self.drive.take()
            it["drive"] = s
            du = st["du"].view[:, :].unsqueeze(1).broadcast_to([P, PAIR, CHUNK])
            t = dve.do(lambda e: e.tensor_tensor(s.view[:, :, :], self.b_bank.view, du, ALU.mult), it["bb_done"], st["du_ready"], *s.free)
            self.b_bank.free, it["drive_done"] = [t], t
            if m == PAIRS - 1:
                st["du"].free = [t]

        def recur(i):
            k, m = items[i]
            it = work[i]
            s = self.h.take()
            it["h"] = s
            for j in range(PAIR):
                n = m * PAIR + j
                start = 0.0 if k % CHUNKS == 0 else self.state[:, n:n + 1]
                t = dve.do(lambda e, j=j, start=start: e.tensor_tensor_scan(s.view[:, j, :], it["decay"].view[:, j, :], it["drive"].view[:, j, :], start,
                                                                           ALU.mult, ALU.add),
                           it["decay_done"], it["drive_done"], self.state_free.get(m), *s.free, signal=(j == PAIR - 1))
            it["decay"].free, it["drive"].free, it["h_done"] = [t], [t], t

        def read_out(i):
            k, m = items[i]
            it = work[i]
            s, total = self.ch.take(), self.ch_sum.take()
            it["sum"] = total
            t = dve.do(lambda e: e.tensor_tensor(s.view[:, :, :], self.c_bank.view, it["h"].view[:, :, :], ALU.mult), it["cc_done"], it["h_done"], *s.free)
            self.c_bank.free = [t]
            kept = dve.do(lambda e: e.tensor_copy(self.state[:, m * PAIR:(m + 1) * PAIR], it["h"].view[:, :, CHUNK - 1]), it["h_done"])
            self.state_free[m] = kept
            it["h"].free = [t, kept]
            t = pool.do(lambda e: e.tensor_tensor(total.view[:, :], s.view[:, 0, :], s.view[:, 1, :], ALU.add), t, *total.free)
            s.free, it["sum_done"] = [t], t

        def add_up(i):
            k, m = items[i]
            it = work.pop(i)
            t = pe.do(lambda e: e.matmul(self.y_bank.view, self.consts.identity[:, :], it["sum"].view[:, :], start=(m == 0), stop=(m == PAIRS - 1)),
                      it["sum_done"], *(self.y_bank.free if m == 0 else []))
            it["sum"].free = [t]
            if m == PAIRS - 1:
                chunks[k]["y_done"] = t
                helpers.insert(0, self.finish_chunk(k, chunks.pop(k)))

        def help_out():
            if helpers:
                if next(helpers[0], "end") == "end":
                    helpers.pop(0)
            elif prep is not None and prep[1] is None:
                try:
                    next(prep[0])
                except StopIteration as e:
                    prep[1] = e.value

        prep = None
        total = len(items)
        for i in range(-AHEAD, total + LAG):
            if i + AHEAD < total:
                k, m = items[i + AHEAD]
                if m == PAIRS // 2:
                    self.load_residual(k, chunks[k])
                if m == 0 and k > 0:
                    while helpers:
                        finish(helpers.pop(0))
                    chunks[k] = prep[1] if prep[1] is not None else finish(prep[0])
                if m == LAG + 2 and k + 1 < BATCH * CHUNKS:
                    prep = [self.prepare(k + 1), None]
            if 0 <= i - 1 < total:
                broadcast(i - 1, "cc", self.c_bank)
            if 0 <= i + 1 < total:
                drive(i + 1)
            if 0 <= i < total:
                recur(i)
            help_out()
            yield
            if i + AHEAD < total:
                decay(i + AHEAD)
            if 0 <= i - 1 < total:
                read_out(i - 1)
            if 0 <= i - LAG < total:
                add_up(i - LAG)
            if i + AHEAD < total:
                broadcast(i + AHEAD, "bb", self.b_bank)
            help_out()
            yield
        while helpers:
            finish(helpers.pop(0))


class Side:

    def __init__(self, thread):
        self.thread, self.ended, self.result = thread, False, None

    def step(self):
        if not self.ended:
            try:
                next(self.thread)
            except StopIteration as e:
                self.ended, self.result = True, e.value

    def end(self):
        while not self.ended:
            self.step()
        return self.result


def along(main, side):
    while True:
        try:
            next(main)
        except StopIteration as e:
            return e.value
        if side is not None:
            side.step()
        yield


class Experts:

    def __init__(self, core, ctx, consts, banks, a, xn_dram, acc_dram, list_dram):
        self.core, self.consts, self.a = core, consts, a
        self.xn_dram, self.acc_dram, self.list_dram = xn_dram, acc_dram, list_dram
        self.banks = Ring([Slot(banks[2][:, :]), Slot(banks[3][:, :])])
        self.xs = core.dma_ring(ctx, "moe_x", 2, [P, GT, D], F32)
        self.xt_hi = core.ring(ctx, "moe_xt_hi", 1, [P, DC, CAPACITY], F32R)
        self.xt_lo = core.ring(ctx, "moe_xt_lo", 1, [P, DC, CAPACITY], F32R)
        self.g = core.ring(ctx, "moe_g", HB, [P, CAPACITY], F32)
        self.u = core.ring(ctx, "moe_u", HB, [P, CAPACITY], F32)
        self.h_hi = core.ring(ctx, "moe_h_hi", 1, [P, HB, CAPACITY], F32R)
        self.h_lo = core.ring(ctx, "moe_h_lo", 1, [P, HB, CAPACITY], F32R)
        self.out = core.dma_ring(ctx, "moe_out", 2, [P, 2, D], F32)
        self.rate = SHARED_RATE
        self.rows = core.sb(ctx, "moe_rows", [P, LISTS * SLOT_TILES], U32)
        self.weight = core.sb(ctx, "moe_weight", [P, LISTS * SLOT_TILES], F32)

    def turn(self, xs, ready):
        core = self.core
        hi, lo = self.xt_hi.take(), self.xt_lo.take()
        for c in range(DC):
            bank = self.banks.take()
            for j in range(GT):
                done = core.pe.do(lambda e, j=j, c=c, bank=bank: e.transpose(
                    bank.view[:, j * P:(j + 1) * P], xs.view[:, j, c * P:(c + 1) * P], self.consts.identity[:, :]),
                    *ready, *bank.free, signal=(j == GT - 1))
            rounded = core.act.do(lambda e, c=c, bank=bank: e.activation(hi.view[:, c, :], bank.view, ACT.Copy), done, *hi.free)
            yield
            split = core.dve.do(lambda e, c=c, bank=bank: e.tensor_tensor(lo.view[:, c, :], bank.view, f32(hi.view[:, c, :]), ALU.subtract), rounded, *hi.free)
            bank.free = [split]
        xs.free = [done]
        yield
        return hi, lo, split

    def up(self, xt, wg, wu):
        core = self.core
        hi, lo, ready = xt
        gs, us = [], []
        for f in range(HB):
            for w, ring, kept in ((wg, self.g, gs), (wu, self.u, us)):
                bank, out = self.banks.take(), ring.take()
                parts = [(c, ws, xs) for c in range(DC) for ws, xs in ((w["hi"], hi), (w["hi"], lo), (w["lo"], hi))]
                for n, (c, ws, xs) in enumerate(parts):
                    done = core.pe.do(lambda e, n=n, c=c, ws=ws, xs=xs, bank=bank, f=f: e.matmul(
                        bank.view, ws[:, c, f * P:(f + 1) * P], xs.view[:, c, :], start=(n == 0), stop=(n == len(parts) - 1)),
                        ready, w["ready"], *bank.free, signal=(n == len(parts) - 1))
                t = core.act.do(lambda e, bank=bank, out=out: e.activation(out.view[:, :], bank.view, ACT.Copy), done, *out.free)
                bank.free = [t]
                kept.append((out, t))
                yield
        hi.free = [done]
        for f, (g, t) in enumerate(gs):
            t = core.act.do(lambda e, g=g: e.activation(g.view[:, :], g.view[:, :], ACT.Gelu), t)
            gs[f] = (g, t)
        return gs, us, done

    def product(self, gs, us):
        core = self.core
        h_hi, h_lo = self.h_hi.take(), self.h_lo.take()
        multiplied = None
        for f in range(HB + 1):
            if multiplied is not None:
                g, t = multiplied
                t = core.act.do(lambda e, g=g, f=f: e.activation(h_hi.view[:, f - 1, :], g.view[:, :], ACT.Copy), t, *h_hi.free)
                split = core.pool.do(lambda e, g=g, f=f: e.tensor_tensor(h_lo.view[:, f - 1, :], g.view[:, :], f32(h_hi.view[:, f - 1, :]), ALU.subtract), t, *h_hi.free)
                g.free = [split]
            if f < HB:
                (g, tg), (u, tu) = gs[f], us[f]
                t = core.pool.do(lambda e, g=g, u=u: e.tensor_tensor(g.view[:, :], g.view[:, :], u.view[:, :], ALU.mult), tg, tu)
                u.free = [t]
                multiplied = (g, t)
            yield
        return h_hi, h_lo, split

    def down(self, h, wd, emit):
        core = self.core
        hi, lo, ready = h
        for pair in range(GT // 2):
            bank = self.banks.take()
            for k in range(2):
                j = 2 * pair + k
                rows = slice(j * P, (j + 1) * P)
                out = bank.view[:, k * D:(k + 1) * D]
                parts = [(f, hs, ws) for f in range(HB) for hs, ws in ((hi, wd["hi"]), (hi, wd["lo"]), (lo, wd["hi"]))]
                for n, (f, hs, ws) in enumerate(parts):
                    done = core.pe.do(lambda e, n=n, f=f, hs=hs, ws=ws, rows=rows, out=out: e.matmul(
                        out, hs.view[:, f, rows], ws[:, f, :], start=(n == 0), stop=(n == len(parts) - 1)),
                        ready, wd["ready"], *bank.free, signal=(n == len(parts) - 1))
                    if n == len(parts) // 2:
                        yield
                yield
            bank.free = [emit(pair, bank.view.rearrange("p (t d) -> p t d", t=2), done)]
        hi.free = [done]
        if "slot" in wd:
            wd["slot"].free = [done]
        return done

    def shared(self):
        core, consts, a = self.core, self.consts, self.a
        pe, act, dve, pool, sp = core.lanes
        with ExitStack() as ctx:
            gate_raw = core.sb(ctx, "gate_raw", [P, DC, EXPERTS], F32)
            gate_hi = core.sb(ctx, "gate_hi", [P, DC, EXPERTS], F32R)
            gate_lo = core.sb(ctx, "gate_lo", [P, DC, EXPERTS], F32R)
            logits = core.ring(ctx, "logits", 2, [P, GT, EXPERTS], F32)
            small = core.ring(ctx, "softmax_small", 2, [P, 2, GT], F32)
            raw = core.dma_ring(ctx, "shared_raw", 3, [P, 1024], F32)
            w = {}
            for name, blocks, cols in (("Ws_gT", DC, HIDDEN), ("Ws_uT", DC, HIDDEN), ("Ws_dT", HB, D)):
                hi = core.sb(ctx, f"{name}_hi", [P, blocks, cols], F32R)
                lo = core.sb(ctx, f"{name}_lo", [P, blocks, cols], F32R)
                s = raw.take()
                v = s.view[:, :].rearrange("p (c n) -> p c n", c=blocks)
                t = sp.dma(s.dma_sem, lambda e, v=v, name=name: e.dma_start(v, a[name].rearrange("(c p) n -> p c n", p=P)), *s.free)
                t = act.do(lambda e, v=v, hi=hi: e.activation(hi[:, :, :], v, ACT.Copy), t)
                t = pool.do(lambda e, v=v, hi=hi, lo=lo: e.tensor_tensor(lo[:, :, :], v, f32(hi[:, :, :]), ALU.subtract), t)
                s.free = [t]
                w[name] = {"hi": hi, "lo": lo, "ready": t}
                yield
            gate_dma = DmaSem(core, "gate_dma")
            t = sp.dma(gate_dma, lambda e: e.dma_start(gate_raw[:, :, :], a["gateT"].rearrange("(c p) n -> p c n", p=P)))
            gate_ready = split_weights_on_pool(core, gate_raw[:, :, :], gate_hi[:, :, :], gate_lo[:, :, :], t)

            def load(group):
                xs = self.xs.take()
                rows = self.xn_dram[group * GROUP:(group + 1) * GROUP, :]
                return xs, sp.dma(xs.dma_sem, lambda e: e.dma_start(xs.view[:, :, :], rows.rearrange("(j p) d -> p j d", p=P)), *xs.free)

            def gate(group, xt):
                hi, lo, ready = xt
                bank = self.banks.take()
                for j in range(GT):
                    rows = slice(j * P, (j + 1) * P)
                    parts = [(c, xs, ws) for c in range(DC) for xs, ws in ((hi, gate_hi), (hi, gate_lo), (lo, gate_hi))]
                    for n, (c, xs, ws) in enumerate(parts):
                        done = pe.do(lambda e, n=n, j=j, c=c, xs=xs, ws=ws, rows=rows: e.matmul(
                            bank.view[:, j * EXPERTS:(j + 1) * EXPERTS], xs.view[:, c, rows], ws[:, c, :], start=(n == 0), stop=(n == len(parts) - 1)),
                            ready, gate_ready, *bank.free, signal=(j == GT - 1 and n == len(parts) - 1))
                lg, sm = logits.take(), small.take()
                psum = bank.view[:, 0:GT * EXPERTS].rearrange("p (j e) -> p j e", j=GT)
                yield
                t = act.do(lambda e: e.activation(lg.view[:, :, :], psum, ACT.Copy), done, *lg.free)
                bank.free = [t]
                wide = lambda row: sm.view[:, row, :].unsqueeze(2).broadcast_to([P, GT, EXPERTS])
                t = dve.do(lambda e: e.tensor_reduce(sm.view[:, 0, :], lg.view[:, :, :], AX_X, ALU.max), t)
                t = dve.do(lambda e: e.tensor_tensor(lg.view[:, :, :], lg.view[:, :, :], wide(0), ALU.subtract), t)
                t = act.do(lambda e: e.activation(lg.view[:, :, :], lg.view[:, :, :], ACT.Exp), t)
                yield
                t = dve.do(lambda e: e.tensor_reduce(sm.view[:, 1, :], lg.view[:, :, :], AX_X, ALU.add), t)
                t = dve.do(lambda e: e.reciprocal(sm.view[:, 1, :], sm.view[:, 1, :]), t)
                b, tile = divmod(group * GT, TILES)
                dst = self.scores[:, b * EXPERTS:(b + 1) * EXPERTS, tile:tile + GT].rearrange("p e j -> p j e")
                t = dve.do(lambda e: e.tensor_tensor(dst, lg.view[:, :, :], wide(1), ALU.mult), t)
                lg.free, self.scored = [t], t

            def keep(group):
                def emit(pair, psum, done):
                    o = self.out.take()
                    t = act.do(lambda e: e.activation(o.view[:, :, :], psum, ACT.Copy), done, *o.free)
                    rows = self.acc_dram[group * GROUP + pair * 2 * P:group * GROUP + (pair + 1) * 2 * P, :]
                    saved = sp.dma(o.dma_sem, lambda e: e.dma_start(rows.rearrange("(j p) d -> p j d", p=P), o.view[:, :, :]), t)
                    o.free = [saved]
                    self.shared_saved[o.dma_sem.sem.name] = saved
                    return t
                return emit

            self.shared_saved = {}
            xs, loaded = load(0)
            products = None
            for group in range(TOKENS // GROUP):
                ahead = load(group + 1) if group + 1 < TOKENS // GROUP else None
                xt = yield from along(self.turn(xs, [loaded]), products)
                yield from along(gate(group, xt), products)
                gs, us, _ = yield from along(self.up(xt, w["Ws_gT"], w["Ws_uT"]), products)
                if group > 0:
                    yield from self.down(products.end(), w["Ws_dT"], keep(group - 1))
                products = Side(self.product(gs, us))
                if ahead is not None:
                    xs, loaded = ahead
            yield from self.down(products.end(), w["Ws_dT"], keep(group))
            self.shared_done = core.pe.last

    def choose(self):
        core, consts = self.core, self.consts
        pe, act, dve, pool, sp = core.lanes
        with ExitStack() as ctx:
            sb = lambda name, shape, dt=F32: core.sb(ctx, name, shape, dt)
            wide = lambda t: t[:, :].unsqueeze(2).broadcast_to([P, LISTS, TILES])
            flat = lambda t: t[:, :, :].rearrange("p l t -> p (l t)")
            full = [P, LISTS, TILES]
            below = sb("below", [P, P])
            reset = sb("reset", full)
            bits, trial, step = sb("bits", [P, LISTS], I32), sb("trial", [P, LISTS], I32), sb("step", [P, LISTS], I32)
            count = sb("count", [P, LISTS])
            need = sb("need", [P, LISTS])
            above, equal, rank, tmp = sb("above", full), sb("equal", full), sb("rank", full), sb("tmp", full)
            row_i, iota_i = sb("row_i", [P, BATCH * TILES], I32), sb("iota_i", [P, COLS32], I32)
            row_f, iota_f = sb("row_f", [P, BATCH * TILES]), sb("iota_f", [P, COLS32])
            left = core.ring(ctx, "onehot_left", 2, [P, TILES, 2 * ROWS16], F32)
            right = Ring([Slot(s.view[:, :, :].rearrange("p a b -> p (a b)").rearrange("p (t c) -> p t c", c=COLS32)) for s in self.xs.slots])
            for s in right.slots:
                s.free = [self.shared_done]
            lists = reset
            first = self.shared_done
            t = pool.do(lambda e: e.affine_select(out=below[:, :], in_=consts.ones[:, :], compare_op=ALU.is_gt, fill=0.0,
                                                  base=0, pattern=[[1, P]], channel_multiplier=-1), first)
            t2 = pool.do(lambda e: e.memset(reset[:, :, :], 1.0), first)
            t2 = pool.do(lambda e: e.memset(reset[:, :, 0:1], 0.0), t2)
            pool.do(lambda e: e.iota(row_i[:, :], [[P, BATCH * TILES]], base=0, channel_multiplier=1), first)
            t3 = pool.do(lambda e: e.iota(iota_i[:, :], [[1, COLS32]], base=0, channel_multiplier=0))
            t3 = dve.do(lambda e: e.tensor_copy(row_f[:, :], row_i[:, :]), t3, first)
            made = dve.do(lambda e: e.tensor_copy(iota_f[:, :], iota_i[:, :]), t2)
            b = dve.do(lambda e: e.memset(bits[:, :], 0))

            def total(mask_sum, ready):
                bank = self.banks.take()
                done = pe.do(lambda e: e.matmul(bank.view[:, 0:LISTS], consts.ones[:, :], mask_sum[:, :], start=True, stop=True), ready, *bank.free)
                return bank, done

            for bit in reversed(range(SCORE_BITS)):
                t = dve.do(lambda e, bit=bit: e.tensor_scalar(trial[:, :], bits[:, :], 1 << bit, None, ALU.bitwise_or), b)
                t = dve.do(lambda e: e.tensor_tensor(tmp[:, :, :], self.scores[:, :, :], wide(trial[:, :].bitcast(F32)), ALU.is_ge), t, self.scored)
                t = dve.do(lambda e: e.tensor_reduce(count[:, :], tmp[:, :, :], AX_X, ALU.add), t)
                bank, done = total(count, t)
                yield
                t = dve.do(lambda e, bank=bank, bit=bit: e.tensor_scalar(step[:, :], bank.view[:, 0:LISTS], float(CAPACITY), float(1 << bit), ALU.is_ge, ALU.mult), done)
                bank.free = [t]
                b = dve.do(lambda e: e.tensor_tensor(bits[:, :], bits[:, :], step[:, :], ALU.bitwise_or), t)
            threshold = bits[:, :].bitcast(F32)
            t = dve.do(lambda e: e.tensor_tensor(above[:, :, :], self.scores[:, :, :], wide(threshold), ALU.is_gt), b)
            e_in = dve.do(lambda e: e.tensor_tensor(equal[:, :, :], self.scores[:, :, :], wide(threshold), ALU.is_equal), b)
            yield
            t = dve.do(lambda e: e.tensor_reduce(count[:, :], above[:, :, :], AX_X, ALU.add), t)
            bank, done = total(count, t)
            t = dve.do(lambda e: e.tensor_scalar(need[:, :], bank.view[:, 0:LISTS], -1.0, float(CAPACITY), ALU.mult, ALU.add), done)
            bank.free = [t]
            needed = t

            def ranks(mask, ready):
                for half in range(2):
                    cols = slice(half * BANK, (half + 1) * BANK)
                    before, totals = self.banks.take(), self.banks.take()
                    d1 = pe.do(lambda e, cols=cols, before=before: e.matmul(before.view, below[:, :], flat(mask)[:, cols], start=True, stop=True), ready, made, *before.free)
                    d2 = pe.do(lambda e, cols=cols, totals=totals: e.matmul(totals.view, consts.ones[:, :], flat(mask)[:, cols], start=True, stop=True), *totals.free)
                    yield
                    t = dve.do(lambda e, cols=cols, totals=totals: e.tensor_tensor_scan(flat(rank)[:, cols], flat(reset)[:, cols], totals.view, 0.0, ALU.mult, ALU.add), d2)
                    t = dve.do(lambda e, cols=cols, totals=totals: e.tensor_tensor(flat(rank)[:, cols], flat(rank)[:, cols], totals.view, ALU.subtract), t)
                    totals.free = [t]
                    t = dve.do(lambda e, cols=cols, before=before: e.tensor_tensor(flat(rank)[:, cols], flat(rank)[:, cols], before.view, ALU.add), t)
                    before.free = [t]
                    yield
                return t

            t = yield from ranks(equal, e_in)
            t = dve.do(lambda e: e.tensor_tensor(tmp[:, :, :], rank[:, :, :], wide(need), ALU.is_lt), t, needed)
            t = dve.do(lambda e: e.tensor_tensor(tmp[:, :, :], tmp[:, :, :], equal[:, :, :], ALU.mult), t)
            t = dve.do(lambda e: e.tensor_tensor(above[:, :, :], above[:, :, :], tmp[:, :, :], ALU.add), t)
            yield
            r = yield from ranks(above, t)
            t = dve.do(lambda e: e.tensor_scalar(tmp[:, :, :], above[:, :, :], -2.0 * SEQ, 2.0 * SEQ, ALU.mult, ALU.add), t)
            t = dve.do(lambda e: e.tensor_tensor(rank[:, :, :], rank[:, :, :], tmp[:, :, :], ALU.add), t, r)
            yield
            as_int = tmp[:, :, :].bitcast(I32)
            t = dve.do(lambda e: e.tensor_copy(as_int, rank[:, :, :]), t)
            t = dve.do(lambda e: e.tensor_scalar(above[:, :, :].bitcast(I32), as_int, 5, None, ALU.logical_shift_right), t)
            t = dve.do(lambda e: e.tensor_copy(equal[:, :, :], above[:, :, :].bitcast(I32)), t)
            yield
            t = dve.do(lambda e: e.tensor_scalar(above[:, :, :].bitcast(I32), as_int, COLS32 - 1, None, ALU.bitwise_and), t)
            ready = dve.do(lambda e: e.tensor_copy(rank[:, :, :], above[:, :, :].bitcast(I32)), t)
            list_row, list_col = equal, rank
            copied = []
            over_tiles = lambda ap, n: ap.unsqueeze(2).broadcast_to([P, TILES, n])
            over_cols = lambda ap, n: ap.unsqueeze(1).broadcast_to([P, TILES, n])
            hot_lists = {}
            for l in range(LISTS + 1):
                yield
                if l < LISTS:
                    A, C = left.take(), right.take()
                    hot = A.view[:, :, ROWS16:2 * ROWS16]
                    t = dve.do(lambda e, l=l, hot=hot: e.tensor_tensor(hot, over_tiles(list_row[:, l, :], ROWS16), over_cols(iota_f[:, 0:ROWS16], ROWS16), ALU.is_equal),
                               ready, made, *A.free)
                    tiles = slice((l // EXPERTS) * TILES, (l // EXPERTS + 1) * TILES)
                    t = pool.do(lambda e, hot=hot, A=A, tiles=tiles: e.tensor_tensor(A.view[:, :, 0:ROWS16], hot, over_tiles(row_f[:, tiles], ROWS16), ALU.mult), t, t3)
                    t = pool.do(lambda e, l=l, hot=hot: e.tensor_tensor(hot, hot, over_tiles(self.scores[:, l, :], ROWS16), ALU.mult), t)
                    t2 = dve.do(lambda e, l=l, C=C: e.tensor_tensor(C.view[:, :, :], over_tiles(list_col[:, l, :], COLS32), over_cols(iota_f[:, :], COLS32), ALU.is_equal),
                                ready, made, *C.free)
                    hot_lists[l] = (A, C, t, t2)
                yield
                if l > 0:
                    A, C, t, t2 = hot_lists.pop(l - 1)
                    bank = self.banks.take()
                    for k in range(TILES):
                        done = pe.do(lambda e, k=k, A=A, C=C, bank=bank: e.matmul(bank.view[0:2 * ROWS16, 0:COLS32], A.view[:, k, :], C.view[:, k, :],
                                                                                 start=(k == 0), stop=(k == TILES - 1)), t, t2, *bank.free, signal=(k == TILES - 1))
                    A.free, C.free = [done], [done]
                    t = act.do(lambda e, l=l, bank=bank: e.activation(lists[0:2 * ROWS16, l - 1, :], bank.view[0:2 * ROWS16, 0:COLS32], ACT.Copy), done)
                    bank.free = [t]
            lists_dma = DmaSem(core, "lists_dma")
            for kind in range(2):
                out = self.list_dram[kind].rearrange("l (a c) -> a l c", a=ROWS16)
                t2 = sp.dma(lists_dma, lambda e, kind=kind, out=out: e.dma_start(out, lists[kind * ROWS16:(kind + 1) * ROWS16, :, :]), t)
            back_dma = DmaSem(core, "lists_back_dma")
            slots = lambda kind: self.list_dram[kind].rearrange("l (p j) -> p l j", p=P)
            as_lists = lambda ap: ap.rearrange("p (l j) -> p l j", j=SLOT_TILES)
            rows_f = tmp[:, 0:SLOT_TILES, :].rearrange("p a b -> p (a b)")
            sp.dma(back_dma, lambda e: e.dma_start(as_lists(rows_f), slots(0)), t2)
            t = sp.dma(back_dma, lambda e: e.dma_start(as_lists(self.weight[:, :]), slots(1)))
            self.chosen = dve.do(lambda e: e.tensor_copy(self.rows[:, :], rows_f), t)
            self.choose_done = [self.chosen, done, core.pool.last, core.act.last]
            yield

    def experts(self):
        core, a = self.core, self.a
        pe, act, dve, pool, sp = core.lanes
        with ExitStack() as ctx:
            raw = core.dma_ring(ctx, "expert_raw", 2, [P, 1024], F32)
            w_hi = core.ring(ctx, "expert_hi", 4, [P, 1024], F32R)
            w_lo = core.ring(ctx, "expert_lo", 4, [P, 1024], F32R)
            for s in raw.slots + w_hi.slots + w_lo.slots + self.xs.slots:
                s.free = list(self.choose_done)
            for s in self.xs.slots + self.out.slots:
                s.dma_sem = DmaSem(core, s.dma_sem.sem.name + "_indirect")
            indirect = lambda col: bass.IndirectOffsetOnAxis(ap=self.rows[:, col:col + 1], axis=0)

            def fetch(name, expert, blocks):
                s = raw.take()
                v = s.view[:, :].rearrange("p (c n) -> p c n", c=blocks)
                t = sp.dma(s.dma_sem, lambda e: e.dma_start(v, a[name][expert].rearrange("(c p) n -> p c n", p=P)), *s.free)
                return s, v, t, blocks

            def weights(fetched):
                s, v, t, blocks = fetched
                hi, lo = w_hi.take(), w_lo.take()
                h, l = (x.view[:, :].rearrange("p (c n) -> p c n", c=blocks) for x in (hi, lo))
                t = act.do(lambda e: e.activation(h, v, ACT.Copy), t, *hi.free)
                t = pool.do(lambda e: e.tensor_tensor(l, v, f32(h), ALU.subtract), t, *hi.free)
                s.free = [t]
                return {"hi": h, "lo": l, "ready": t, "slot": hi}

            order = [(expert, b) for expert in range(EXPERTS) for b in range(BATCH)]
            gathered = {}

            def gather(n):
                expert, b = order[n]
                xs = self.xs.take()
                for j in range(SLOT_TILES):
                    t = pool.dma(xs.dma_sem, lambda e, j=j: e.indirect_dma_start(
                        xs.view[:, j, :], None, self.xn_dram, indirect((b * EXPERTS + expert) * SLOT_TILES + j)), self.chosen, *xs.free)
                    gathered[n] = (xs, t)
                    yield

            def background(n, before):
                expert, b = order[n]
                h = (yield from self.product(*before)) if before is not None else None
                if n + 1 < len(order):
                    yield from gather(n + 1)
                if b == 0:
                    w[expert]["d"] = weights(fetched["d"])
                elif expert + 1 < EXPERTS:
                    w[expert + 1] = {"g": weights(fetched["g"])}
                yield
                return h

            added = {}

            def scatter(l, expert):
                b = l // EXPERTS

                def emit(pair, psum, done):
                    o = self.out.take()
                    for k in range(2):
                        col = l * SLOT_TILES + 2 * pair + k
                        t = act.do(lambda e, k=k, col=col: e.activation(o.view[:, k, :], psum[:, k, :], ACT.Copy, scale=self.weight[:, col:col + 1]), done, *o.free)
                    before = [x for key, x in added.items() if key[0] == b and key[1] < expert]
                    for k in range(2):
                        col = l * SLOT_TILES + 2 * pair + k
                        s = pool.dma(o.dma_sem, lambda e, k=k, col=col: e.indirect_dma_start(
                            self.acc_dram, indirect(col), o.view[:, k, :], None, compute_op=ALU.add),
                            t, *before, *self.shared_saved.values())
                    o.free = [s]
                    added[b, expert, pair] = s
                    for key in [key for key in added if key[0] == b and key[1] < expert - 1]:
                        added.pop(key)
                    return t
                return emit

            w = {0: {}}
            fetched = {"g": fetch("WgT", 0, DC), "u": fetch("WuT", 0, DC)}
            for kind in "gu":
                w[0][kind] = weights(fetched[kind])
            fetched["d"] = fetch("WdT", 0, HB)
            finish(gather(0))
            before, halves = None, None
            for n, (expert, b) in enumerate(order):
                more = b == BATCH - 1 and expert + 1 < EXPERTS
                if more:
                    fetched = {"g": fetch("WgT", expert + 1, DC), "u": fetch("WuT", expert + 1, DC)}
                side = Side(background(n, halves))
                xs, loaded = gathered.pop(n)
                xt = yield from along(self.turn(xs, [loaded]), side)
                gs, us, up_done = yield from along(self.up(xt, w[expert]["g"], w[expert]["u"]), side)
                h = side.end()
                if b == BATCH - 1:
                    w[expert]["g"]["slot"].free = [up_done]
                    w[expert]["u"]["slot"].free = [up_done]
                if before is not None:
                    e0, b0 = before
                    yield from self.down(h, w[e0]["d"], scatter(b0 * EXPERTS + e0, e0))
                    if b0 == BATCH - 1:
                        w.pop(e0)
                if more:
                    w[expert + 1]["u"] = weights(fetched["u"])
                    fetched["d"] = fetch("WdT", expert + 1, HB)
                before, halves = (expert, b), (gs, us)
            h = yield from self.product(*halves)
            yield from self.down(h, w[expert]["d"], scatter(b * EXPERTS + expert, expert))

    def thread(self):
        with ExitStack() as until_chosen:
            self.scores = self.core.sb(until_chosen, "moe_scores", [P, LISTS, TILES], F32)
            yield from self.shared()
            self.rate = CHOOSE_RATE
            yield from self.choose()
        self.rate = EXPERTS_RATE
        yield from self.experts()


def layer1(core, consts, a, x1_dram, xn_dram, s_dram, acc_dram, list_dram, out_dram):
    with ExitStack() as stage:
        w = ScanWeights(core, stage, consts, a)
        pair_banks = [stage.enter_context(core.nc.psum_tensor(f"state_pair_{what}", [P, PAIR, CHUNK], F32)) for what in "BC"]
        banks = [stage.enter_context(core.nc.psum_tensor(f"layer1_bank{i}", [P, BANK], F32)) for i in range(4)]
        scan = SelectiveScan(core, stage, consts, w, banks, pair_banks, xn_dram, s_dram)
        moe = Experts(core, stage, consts, banks, a, xn_dram, acc_dram, list_dram)
        scan_steps, moe_steps = scan.thread(), moe.thread()
        due = 0.0
        for _ in scan_steps:
            due += moe.rate
            while due >= 1.0:
                next(moe_steps, None)
                due -= 1.0
        finish(moe_steps)
        core.hand_over()
    combine(core, x1_dram, s_dram, acc_dram, out_dram)


def combine(core, x1_dram, s_dram, moe_dram, out_dram):
    pe, act, dve, pool, sp = core.lanes
    with ExitStack() as ctx:
        x_ring = core.dma_ring(ctx, "final_x", 5, [P, GT, D], F32)
        s_ring = core.dma_ring(ctx, "final_s", 4, [P, GT, D], F32)
        m_ring = core.dma_ring(ctx, "final_m", 4, [P, GT, D], F32)
        e_ring = core.ring(ctx, "final_e", 3, [P, GT, D], F32)
        groups = TOKENS // GROUP
        rows = lambda dram, g: dram[g * GROUP:(g + 1) * GROUP, :].rearrange("(p j) d -> p j d", p=P)
        v = lambda slot: slot.view[:, :, :]

        def load(g):
            x, s, m = x_ring.take(), s_ring.take(), m_ring.take()
            bring = lambda slot, dram: sp.dma(slot.dma_sem, lambda q: q.dma_start(v(slot), rows(dram, g)), *slot.free)
            return (m, bring(m, moe_dram)), (s, bring(s, s_dram)), (x, bring(x, x1_dram))

        def add(g, loaded):
            (m, tm), (s, ts), (x, tx) = loaded
            e = e_ring.take()
            t = act.do(lambda q: q.activation(v(e), v(m), ACT.Silu), tm, *e.free)
            m.free = [t]
            t = dve.do(lambda q: q.tensor_tensor(v(e), v(e), v(s), ALU.mult), t, ts)
            s.free = [t]
            t = dve.do(lambda q: q.tensor_tensor(v(x), v(x), v(e), ALU.add), t, tx)
            e.free = [t]
            x.free = [sp.dma(x.dma_sem, lambda q: q.dma_start(rows(out_dram, g), v(x)), t)]

        loaded = [load(g) for g in range(3)]
        for g in range(groups):
            add(g, loaded.pop(0))
            if g + 3 < groups:
                loaded.append(load(g + 3))
        core.hand_over()


LAYER0_INPUTS = ("x", "qkv", "woT", "out_b", "w1", "w1T", "b1", "w2", "w2T", "b2")
LAYER1_INPUTS = ("ln_gamma", "ln_beta", "W_up", "b_up", "conv_w", "conv_b", "W_delta", "b_delta", "W_B", "W_C", "A_log", "D",
                 "W_down", "b_down", "gateT", "WgT", "WuT", "WdT", "Ws_gT", "Ws_uT", "Ws_dT")


def two_layers(nc, a, out_dram):
    scratch = lambda name, shape: nc.dram_tensor(name, shape, F32, kind="Internal").ap()
    q_dram = scratch("q_scratch", [BATCH * GROUPS, P, DC, GROUP])
    g_dram = scratch("g_scratch", [TOKENS, D])
    x1_dram = scratch("x1_scratch", [TOKENS, D])
    xn1_dram = scratch("xn1_scratch", [TOKENS, D])
    s_dram = scratch("s_scratch", [TOKENS, D])
    moe_dram = scratch("moe_scratch", [TOKENS, D])
    list_dram = scratch("list_scratch", [2, LISTS, CAPACITY])
    with ExitStack() as ctx:
        core = Core(nc, ctx)
        consts = Constants(core, ctx)
        with ExitStack() as layer0:
            w = Layer0Weights(core, layer0, consts, a)
            kv = KeysValues(core, layer0)
            for b in range(BATCH):
                binary_ffn_and_qkv(core, consts, w, kv, b, a["x"], q_dram, g_dram)
                attention(core, consts, w, kv, b, a["x"], q_dram, g_dram, x1_dram, xn1_dram)
        layer1(core, consts, a, x1_dram, xn1_dram, s_dram, moe_dram, list_dram, out_dram)
        core.sp.do(lambda e: e.drain())
        core.run()


def kernel(**inputs):
    import numpy as np
    import concourse.bacc as bacc
    from concourse.bass_utils import run_bass_kernel_spmd

    rest = slice(D // 4, 3 * D // 4)
    order = np.concatenate([np.arange(0, D // 4), np.arange(3 * D // 4, D), np.arange(rest.start, rest.stop)])
    l0a, l0f = (lambda n: np.asarray(inputs["L0_attn_" + n])), (lambda n: np.asarray(inputs["L0_ffn_" + n]))
    l1a, l1f = (lambda n: np.asarray(inputs["L1_attn_" + n])), (lambda n: np.asarray(inputs["L1_ffn_" + n]))
    arrays = {
        "x": l0a("x").reshape(TOKENS, D)[:, order],
        "qkv": l0a("weight_qkv")[order],
        "woT": l0a("out_w").T[:, order],
        "out_b": l0a("out_b")[order],
        "w1": l0f("w1")[:, order],
        "w1T": l0f("w1").T[order],
        "b1": l0f("b1"),
        "w2": l0f("w2")[order],
        "w2T": l0f("w2").T[:, order],
        "b2": l0f("b2")[order],
        "ln_gamma": l1a("ln_gamma")[order],
        "ln_beta": l1a("ln_beta")[order],
        "W_up": l1a("W_up")[order],
        "b_up": l1a("b_up"),
        "conv_w": l1a("conv_w")[:, 0, :],
        "conv_b": l1a("conv_b"),
        "W_delta": l1a("W_delta"),
        "b_delta": l1a("b_delta"),
        "W_B": l1a("W_B"),
        "W_C": l1a("W_C"),
        "A_log": l1a("A_log"),
        "D": l1a("D"),
        "W_down": l1a("W_down")[:, order],
        "b_down": l1a("b_down")[order],
        "gateT": l1f("gate_w")[:, order].T,
        "WgT": l1f("Wg")[:, :, order].transpose(0, 2, 1),
        "WuT": l1f("Wu")[:, :, order].transpose(0, 2, 1),
        "WdT": l1f("Wd")[:, order, :].transpose(0, 2, 1),
        "Ws_gT": l1f("Ws_g")[:, order].T,
        "Ws_uT": l1f("Ws_u")[:, order].T,
        "Ws_dT": l1f("Ws_d")[order].T,
    }
    nc = bacc.Bacc("TRN2", target_bir_lowering=False, num_devices=1)
    a = {}
    for name in LAYER0_INPUTS + LAYER1_INPUTS:
        arrays[name] = np.ascontiguousarray(arrays[name])
        a[name] = nc.dram_tensor(name, arrays[name].shape, mybir.dt.from_np(arrays[name].dtype), kind="ExternalInput").ap()
    out_dram = nc.dram_tensor("x2", [TOKENS, D], F32, kind="ExternalOutput").ap()
    two_layers(nc, a, out_dram)
    result = run_bass_kernel_spmd(nc, [arrays], core_ids=[0]).results[0]["x2"]
    out = np.empty_like(result)
    out[:, order] = result
    return out.reshape(BATCH, SEQ, D)
```
